# Optimizing a Trainium2 kernel written in Bass

```python
import numpy as np
import jax
import jax.numpy as jnp

def _softmax(x, axis=-1):
    return jax.nn.softmax(x, axis=axis)

def _gelu(x):
    return jax.nn.gelu(x, approximate=True)

def _silu(x):
    return jax.nn.silu(x)

def _sigmoid(x):
    return jax.nn.sigmoid(x)

def _layernorm(x, axis=-1, eps=1e-05):
    m = jnp.mean(x, axis=axis, keepdims=True)
    v = jnp.var(x, axis=axis, keepdims=True)
    return (x - m) / jnp.sqrt(v + eps)

def _scatter_add(tgt, idx, src, axis=0):
    return tgt.at[idx].add(src)

def _segment_sum(src, seg, n):
    return jax.ops.segment_sum(src, seg, n)
kernel_name = 'mk_conv_seq_d2_conv_nchw512_r2_df1198'

def setup_inputs(seed: int=0):
    np.random.seed(seed)
    _w = jnp.asarray

    def _rec_inputs():
        import jax
        import jax.numpy as jnp
        _gk = jax.random.key(seed)
        x = 7.22e-05 + 1 * jax.random.normal(jax.random.fold_in(_gk, 1), (4, 256, 32, 32), jnp.float32)
        return x
    x = _rec_inputs()

    def _L0_conv_setup():
        import jax, jax.numpy as jnp
        import numpy as np
        from jax import lax
        IN_CH = 256
        OUT_CH = 256
        HEAD_DIM = 8
        NUM_HEADS = IN_CH // HEAD_DIM
        INNER = NUM_HEADS * HEAD_DIM
        KSIZE = 5
        EPS = 1e-15
        BN_EPS = 1e-05
        DN = ('NCHW', 'OIHW', 'NCHW')

        def _forward(hidden_states, wq, wk, wv, dw_kernel, pw_kernel, proj_kernel, bn_gamma, bn_beta, bn_mean, bn_var):
            x = hidden_states
            B, _, H, W = x.shape
            h = jnp.moveaxis(x, 1, -1)
            q = h @ wq.T
            k = h @ wk.T
            v = h @ wv.T
            qkv = jnp.moveaxis(jnp.concatenate([q, k, v], axis=-1), -1, 1)
            dw = lax.conv_general_dilated(qkv, dw_kernel, (1, 1), 'SAME', feature_group_count=3 * INNER, dimension_numbers=DN)
            pw = lax.conv_general_dilated(dw, pw_kernel, (1, 1), 'VALID', feature_group_count=3 * NUM_HEADS, dimension_numbers=DN)
            qkv_all = jnp.concatenate([qkv, pw], axis=1)
            N = H * W
            d = HEAD_DIM
            f = qkv_all.astype(jnp.float32).reshape(B, -1, 3 * d, N)
            query = jax.nn.relu(f[:, :, :d])
            key_ = jax.nn.relu(f[:, :, d:2 * d])
            value = f[:, :, 2 * d:]
            value_pad = jnp.concatenate([value, jnp.ones_like(value[:, :, :1])], axis=2)
            scores = jnp.einsum('bhdn,bhen->bhde', value_pad, key_)
            out = jnp.einsum('bhde,bhen->bhdn', scores, query)
            out = out[:, :, :-1] / (out[:, :, -1:] + EPS)
            out = out.reshape(B, -1, H, W).astype(qkv_all.dtype)
            y = lax.conv_general_dilated(out, proj_kernel, (1, 1), 'VALID', dimension_numbers=DN)
            inv = bn_gamma / jnp.sqrt(bn_var + BN_EPS)
            y = y * inv[None, :, None, None] + (bn_beta - bn_mean * inv)[None, :, None, None]
            return y + x
        key = jax.random.key(seed)
        ks = jax.random.split(key, 10)
        s = 0.02
        return {'hidden_states': jax.random.normal(ks[0], (4, IN_CH, 32, 32), jnp.float32), 'wq': jax.random.normal(ks[1], (INNER, IN_CH), jnp.float32) * s, 'wk': jax.random.normal(ks[2], (INNER, IN_CH), jnp.float32) * s, 'wv': jax.random.normal(ks[3], (INNER, IN_CH), jnp.float32) * s, 'dw_kernel': jax.random.normal(ks[4], (3 * INNER, 1, KSIZE, KSIZE), jnp.float32) * s, 'pw_kernel': jax.random.normal(ks[5], (3 * INNER, HEAD_DIM, 1, 1), jnp.float32) * s, 'proj_kernel': jax.random.normal(ks[6], (OUT_CH, 2 * INNER, 1, 1), jnp.float32) * s, 'bn_gamma': jnp.ones((OUT_CH,), jnp.float32), 'bn_beta': jnp.zeros((OUT_CH,), jnp.float32), 'bn_mean': jnp.zeros((OUT_CH,), jnp.float32), 'bn_var': jnp.ones((OUT_CH,), jnp.float32)}
    _L0_conv_all = _L0_conv_setup()
    _L0_conv_in = {k: v for k, v in _L0_conv_all.items() if k in ('wq', 'wk', 'wv', 'dw_kernel', 'pw_kernel', 'proj_kernel', 'bn_gamma', 'bn_beta', 'bn_mean', 'bn_var')}
    del _L0_conv_all

    def _L1_conv_setup():
        import jax, jax.numpy as jnp
        import numpy as np
        EPS = 1e-05

        def mean_std_norm(x):
            mean = jnp.mean(x, axis=(2, 3), keepdims=True)
            var = jnp.var(x, axis=(2, 3), keepdims=True)
            return (x - mean) / jnp.sqrt(var + EPS)

        def conv1x1(x, w, b):
            return jnp.einsum('oc,bchw->bohw', w, x) + b[None, :, None, None]
        key = jax.random.key(seed)
        ks = jax.random.split(key, 9)
        C = 256
        s = 1.0 / np.sqrt(C)
        inp = {'content_feat': jax.random.normal(ks[0], (4, C, 32, 32), dtype=jnp.float32), 'f_w': jax.random.normal(ks[1], (C, C), dtype=jnp.float32) * s, 'f_b': jnp.zeros((C,), dtype=jnp.float32), 'g_w': jax.random.normal(ks[2], (C, C), dtype=jnp.float32) * s, 'g_b': jnp.zeros((C,), dtype=jnp.float32), 'h_w': jax.random.normal(ks[3], (C, C), dtype=jnp.float32) * s, 'h_b': jnp.zeros((C,), dtype=jnp.float32), 'o_w': jax.random.normal(ks[4], (C, C), dtype=jnp.float32) * s, 'o_b': jnp.zeros((C,), dtype=jnp.float32)}
        return inp
    _L1_conv_all = _L1_conv_setup()
    _L1_conv_in = {k: v for k, v in _L1_conv_all.items() if k in ('f_w', 'f_b', 'g_w', 'g_b', 'h_w', 'h_b', 'o_w', 'o_b')}
    del _L1_conv_all
    return {'x': x, 'L0_conv_wq': _L0_conv_in['wq'], 'L0_conv_wk': _L0_conv_in['wk'], 'L0_conv_wv': _L0_conv_in['wv'], 'L0_conv_dw_kernel': _L0_conv_in['dw_kernel'], 'L0_conv_pw_kernel': _L0_conv_in['pw_kernel'], 'L0_conv_proj_kernel': _L0_conv_in['proj_kernel'], 'L0_conv_bn_gamma': _L0_conv_in['bn_gamma'], 'L0_conv_bn_beta': _L0_conv_in['bn_beta'], 'L0_conv_bn_mean': _L0_conv_in['bn_mean'], 'L0_conv_bn_var': _L0_conv_in['bn_var'], 'L1_conv_f_w': _L1_conv_in['f_w'], 'L1_conv_f_b': _L1_conv_in['f_b'], 'L1_conv_g_w': _L1_conv_in['g_w'], 'L1_conv_g_b': _L1_conv_in['g_b'], 'L1_conv_h_w': _L1_conv_in['h_w'], 'L1_conv_h_b': _L1_conv_in['h_b'], 'L1_conv_o_w': _L1_conv_in['o_w'], 'L1_conv_o_b': _L1_conv_in['o_b']}

def reference(x, L0_conv_wq, L0_conv_wk, L0_conv_wv, L0_conv_dw_kernel, L0_conv_pw_kernel, L0_conv_proj_kernel, L0_conv_bn_gamma, L0_conv_bn_beta, L0_conv_bn_mean, L0_conv_bn_var, L1_conv_f_w, L1_conv_f_b, L1_conv_g_w, L1_conv_g_b, L1_conv_h_w, L1_conv_h_b, L1_conv_o_w, L1_conv_o_b):
    import jax
    import jax.numpy as jnp

    def _L0_conv_ref(hidden_states, wq, wk, wv, dw_kernel, pw_kernel, proj_kernel, bn_gamma, bn_beta, bn_mean, bn_var):
        import jax, jax.numpy as jnp
        import numpy as np
        from jax import lax
        IN_CH = 256
        OUT_CH = 256
        HEAD_DIM = 8
        NUM_HEADS = IN_CH // HEAD_DIM
        INNER = NUM_HEADS * HEAD_DIM
        KSIZE = 5
        EPS = 1e-15
        BN_EPS = 1e-05
        DN = ('NCHW', 'OIHW', 'NCHW')

        def _forward(hidden_states, wq, wk, wv, dw_kernel, pw_kernel, proj_kernel, bn_gamma, bn_beta, bn_mean, bn_var):
            x = hidden_states
            B, _, H, W = x.shape
            h = jnp.moveaxis(x, 1, -1)
            q = h @ wq.T
            k = h @ wk.T
            v = h @ wv.T
            qkv = jnp.moveaxis(jnp.concatenate([q, k, v], axis=-1), -1, 1)
            dw = lax.conv_general_dilated(qkv, dw_kernel, (1, 1), 'SAME', feature_group_count=3 * INNER, dimension_numbers=DN)
            pw = lax.conv_general_dilated(dw, pw_kernel, (1, 1), 'VALID', feature_group_count=3 * NUM_HEADS, dimension_numbers=DN)
            qkv_all = jnp.concatenate([qkv, pw], axis=1)
            N = H * W
            d = HEAD_DIM
            f = qkv_all.astype(jnp.float32).reshape(B, -1, 3 * d, N)
            query = jax.nn.relu(f[:, :, :d])
            key_ = jax.nn.relu(f[:, :, d:2 * d])
            value = f[:, :, 2 * d:]
            value_pad = jnp.concatenate([value, jnp.ones_like(value[:, :, :1])], axis=2)
            scores = jnp.einsum('bhdn,bhen->bhde', value_pad, key_)
            out = jnp.einsum('bhde,bhen->bhdn', scores, query)
            out = out[:, :, :-1] / (out[:, :, -1:] + EPS)
            out = out.reshape(B, -1, H, W).astype(qkv_all.dtype)
            y = lax.conv_general_dilated(out, proj_kernel, (1, 1), 'VALID', dimension_numbers=DN)
            inv = bn_gamma / jnp.sqrt(bn_var + BN_EPS)
            y = y * inv[None, :, None, None] + (bn_beta - bn_mean * inv)[None, :, None, None]
            return y + x
        return _forward(hidden_states, wq, wk, wv, dw_kernel, pw_kernel, proj_kernel, bn_gamma, bn_beta, bn_mean, bn_var)

    def _L1_conv_ref(content_feat, f_w, f_b, g_w, g_b, h_w, h_b, o_w, o_b):
        import jax, jax.numpy as jnp
        import numpy as np
        EPS = 1e-05

        def mean_std_norm(x):
            mean = jnp.mean(x, axis=(2, 3), keepdims=True)
            var = jnp.var(x, axis=(2, 3), keepdims=True)
            return (x - mean) / jnp.sqrt(var + EPS)

        def conv1x1(x, w, b):
            return jnp.einsum('oc,bchw->bohw', w, x) + b[None, :, None, None]
        B, C, H, W = content_feat.shape
        HW = H * W
        norm = mean_std_norm(content_feat)
        F_Fc = conv1x1(norm, f_w, f_b).reshape(B, C, HW).transpose(0, 2, 1)
        G_Fs = conv1x1(norm, g_w, g_b).reshape(B, C, HW)
        energy = jnp.einsum('bnc,bcm->bnm', F_Fc, G_Fs)
        attention = jax.nn.softmax(energy, axis=-1)
        H_Fs = conv1x1(content_feat, h_w, h_b).reshape(B, C, HW)
        out = jnp.einsum('bcn,bmn->bcm', H_Fs, attention).reshape(B, C, H, W)
        out = conv1x1(out, o_w, o_b)
        return out + content_feat

    def _gn(v, G=32, eps=1e-05):
        B_, C_, H_, W_ = v.shape
        g = v.reshape(B_, G, C_ // G, H_, W_)
        m = jnp.mean(g, axis=(2, 3, 4), keepdims=True)
        s = jnp.var(g, axis=(2, 3, 4), keepdims=True)
        return ((g - m) / jnp.sqrt(s + eps)).reshape(v.shape)

    def _ln_c(v, eps=1e-06):
        m = jnp.mean(v, axis=1, keepdims=True)
        s = jnp.var(v, axis=1, keepdims=True)
        return (v - m) / jnp.sqrt(s + eps)

    def _ln_t(v, eps=1e-05):
        m = jnp.mean(v, axis=-1, keepdims=True)
        s = jnp.var(v, axis=-1, keepdims=True)
        return (v - m) / jnp.sqrt(s + eps)

    def _to_tokens(v):
        B_, C_, H_, W_ = v.shape
        return v.reshape(B_, C_, H_ * W_).transpose(0, 2, 1)

    def _from_tokens(t, like):
        B_, C_, H_, W_ = like.shape
        return t.transpose(0, 2, 1).reshape(B_, C_, H_, W_)
    x = _L0_conv_ref(x, L0_conv_wq, L0_conv_wk, L0_conv_wv, L0_conv_dw_kernel, L0_conv_pw_kernel, L0_conv_proj_kernel, L0_conv_bn_gamma, L0_conv_bn_beta, L0_conv_bn_mean, L0_conv_bn_var)
    x = _L1_conv_ref(x, L1_conv_f_w, L1_conv_f_b, L1_conv_g_w, L1_conv_g_b, L1_conv_h_w, L1_conv_h_b, L1_conv_o_w, L1_conv_o_b)
    return x

_drawn_inputs = setup_inputs


def setup_inputs(seed=0):
    import zlib

    import numpy as np

    out = dict(_drawn_inputs(seed))
    spreads = {'L0_conv_bn_gamma': (1.0, 0.6),
     'L0_conv_bn_beta': (0.0, 0.1),
     'L0_conv_bn_mean': (0.0, 0.1),
     'L0_conv_bn_var': (1.0, 0.6),
     'L1_conv_f_b': (0.0, 0.1),
     'L1_conv_g_b': (0.0, 0.8),
     'L1_conv_h_b': (0.0, 0.1),
     'L1_conv_o_b': (0.0, 0.1)}
    factors = {'L0_conv_wq': 4.527,
     'L0_conv_wk': 4.615,
     'L0_conv_wv': 4.506,
     'L0_conv_dw_kernel': 8.0,
     'L0_conv_pw_kernel': 8.0,
     'L0_conv_proj_kernel': 2.697}
    for name, (base, spread) in spreads.items():
        noise = np.random.default_rng([zlib.crc32(name.encode()), seed]).standard_normal(out[name].shape)
        drawn = base * np.exp(spread * noise) if base else spread * noise
        out[name] = jnp.asarray(drawn.astype(out[name].dtype))
    for name, factor in factors.items():
        out[name] = (out[name] * factor).astype(out[name].dtype)
    return out
```

```python
from contextlib import ExitStack

import numpy as np
import concourse.bass as bass
from concourse import mybir

ALU = mybir.AluOpType
ACT = mybir.ActivationFunctionType
AX = mybir.AxisListType
F32 = mybir.dt.float32
F32R = mybir.dt.float32r

P = 128
B = 4
C = 256
SIDE = 32
N = SIDE * SIDE
CK = C // P
HALF = N // 2
NB = N // P
D = 8
HEADS = C // D
HPT = P // D
TILES = 3 * CK
TAPS = 5
PAD = TAPS // 2
ROW = SIDE + PAD
IMG = (SIDE + 2 * PAD) * ROW + PAD
IMG += -IMG % 4
KV0 = PAD * ROW
RB = -(-SIDE * ROW // P)
SCW = P + 1
SDW = P + HPT
ATT_EPS = 1e-15
BN_EPS = 1e-5
NORM_EPS = 1e-5
NTAPS = TAPS * TAPS
CONV_STEPS = TILES * NTAPS

A_BANKS = 4
D_BANKS = 2
A_RAW, A_KVT, A_PWQ, A_PWKV, A_TR, A_HT = 2 * TILES, RB, 2 * CK, NB, 2 * CK, NB // 2
D_SC, D_OUT, D_PROJ, D_FG = 1, NB, 2 * CK, 4 * CK
A_FIRST = A_RAW + A_KVT + A_TR
A_BODY = A_FIRST + A_PWQ + A_PWKV + A_TR + A_HT
D_FIRST = D_SC + D_OUT
D_BODY = 2 * D_FIRST + D_PROJ + D_FG


def conv_seq_kernel(nc, x, wqkv, dw, pw, proj, bn, fgw, hw, ow, l1b, masks, out):
    with ExitStack() as ctx:
        def sb(name, shape, dt=F32):
            return ctx.enter_context(nc.sbuf_tensor(name, shape, dt))

        def sem(name):
            return ctx.enter_context(nc.semaphore(name))

        x_in = sb("x_in", [P, CK, N])
        hi = sb("hi", [P, CK, N], F32R)
        lo = sb("lo", [P, CK, N], F32R)
        raw = sb("raw", [P, TILES, IMG])
        conv = sb("conv", [P, TILES, N])
        qp = sb("qp", [P, 4, N])
        kv = sb("kv", [P, RB * C + NB * C])
        vt = sb("vt", [P, RB, CK, SCW + 1])
        sd = sb("sd", [P, CK, SDW])
        oc = sb("oc", [P, 4, N])
        x1 = sb("x1", [P, CK, N])
        f_hi = sb("f_hi", [P, CK, N], F32R)
        f_lo = sb("f_lo", [P, CK, N], F32R)
        g_hi = sb("g_hi", [P, CK, N], F32R)
        g_lo = sb("g_lo", [P, CK, N], F32R)
        wqkv_hi = sb("wqkv_hi", [P, CK, TILES * P], F32R)
        wqkv_lo = sb("wqkv_lo", [P, CK, TILES * P], F32R)
        fg_hi = sb("fg_hi", [P, 2, CK, C], F32R)
        fg_lo = sb("fg_lo", [P, 2, CK, C], F32R)
        pw_sb = sb("pw_sb", [P, TILES, P])
        proj_sb = sb("proj_sb", [P, 2 * CK, C])
        dw_sb = sb("dw_sb", [P, TILES, NTAPS])
        oh_w = sb("oh_w", [P, CK, C])
        mask_sb = sb("mask_sb", [P, 2 * P + HPT])
        bn_sb = sb("bn_sb", [P, 4, CK])
        l1b_sb = sb("l1b_sb", [P, 4, CK])
        small = sb("small", [P, 12, 8])

        ident = mask_sb[:, 0:P]
        mask_blk = mask_sb[:, P:2 * P]
        mask_head = mask_sb[:, 2 * P:2 * P + HPT]
        kt = kv[:, 0:RB * C].rearrange("p (j c) -> p j c", c=C)
        ot = kv[:, RB * C:].rearrange("p (j c) -> p j c", c=C)
        pt = kv[:, 0:NB * HALF].rearrange("p (j q) -> p j q", q=HALF)
        ht = oc[:, 2:4, :].rearrange("p a (j c) -> p (a j) c", c=C)
        nf = qp[:, 0:CK, :]
        raw_img = raw[:, :, 0:(SIDE + 2 * PAD) * ROW].rearrange("p t (y x) -> p t y x", x=ROW)
        wqkv_st = conv[:, 0:2, :].rearrange("p a n -> p (a n)")[:, 0:CK * TILES * P].rearrange(
            "p (k m) -> p k m", k=CK)
        fg_st = conv[:, 2, :].rearrange("p (w k m) -> p w k m", w=2, k=CK)
        hw_st = conv[:, 3, 0:CK * C].rearrange("p (k m) -> p k m", k=CK)
        ow_st = conv[:, 3, CK * C:].rearrange("p (k m) -> p k m", k=CK)
        gamma, beta, mean, var = (bn_sb[:, i, :] for i in range(4))
        f_b, g_b, h_b, o_b = (l1b_sb[:, i, :] for i in range(4))
        bn_ve, bn_scale, bn_shift, minus_half, oh_b = (small[:, i, 0:CK] for i in range(5))
        neg_max, row_sum, row_rcp = (small[:, i, :] for i in (5, 6, 7))
        stat_ve, stat_rstd = (small[:, i, 0:CK] for i in (8, 9))
        bn_tmp = small[:, 10, 0:CK]
        stats = sb("stats", [P, CK, 2, 6])
        mv = sb("mv", [P, CK, 2])
        den = sb("den", [P, 2, CK * HPT])

        ps = ctx.enter_context(nc.psum_tensor("ps", [P, 8, 512], F32))
        acc = ps[:, 6:8, :].rearrange("p a n -> p (a n)").rearrange("p (y x) -> p y x", x=SIDE)

        w_loaded = sem("w_loaded")
        x_loaded = sem("x_loaded")
        res_loaded = sem("res_loaded")
        stored = sem("stored")
        prep_act = sem("prep_act")
        prep_dve = sem("prep_dve")
        prep_pe = sem("prep_pe")
        prep_pool = sem("prep_pool")
        hi_ready = sem("hi_ready")
        lo_ready = sem("lo_ready")
        a_full = sem("a_full")
        a_free = sem("a_free")
        d_full = sem("d_full")
        d_free = sem("d_free")
        conv_dve = sem("conv_dve")
        dve_step = sem("dve_step")
        res_biased = sem("res_biased")
        var_ready = sem("var_ready")
        rstd_ready = sem("rstd_ready")
        norm_ready = sem("norm_ready")
        norm_hi = sem("norm_hi")
        norm_lo = sem("norm_lo")
        fg_hi_ready = sem("fg_hi_ready")
        e_full = sem("e_full")
        max_ready = sem("max_ready")
        exp_done = sem("exp_done")
        rcp_ready = sem("rcp_ready")
        p_ready = sem("p_ready")
        t_full = sem("t_full")
        t_free = sem("t_free")
        pv_full = sem("pv_full")
        pv_free = sem("pv_free")

        STEPS_OUT = 2 * NB
        STEPS_BODY = 2 * STEPS_OUT + 2
        PREP_STEPS = 4

        def a_base(b):
            return A_FIRST + A_BODY * b

        def d_base(b):
            return D_FIRST + D_BODY * b

        def a_offsets(with_next):
            o, at = {}, 0
            for name, n in (("pwq", A_PWQ), ("pwkv", A_PWKV), ("raw", A_RAW * with_next), ("kvt", A_KVT * with_next),
                            ("tr_pw", A_TR), ("tr_raw", A_TR * with_next), ("ht", A_HT)):
                o[name] = at
                at += n
            return o

        def d_offsets(with_next):
            o, at = {}, 0
            for name, n in (("sc_pw", D_SC), ("out_pw", D_OUT), ("sc_raw", D_SC * with_next),
                            ("out_raw", D_OUT * with_next), ("proj", D_PROJ), ("fg", D_FG)):
                o[name] = at
                at += n
            return o

        FIRST_A = {"raw": 0, "kvt": A_RAW, "tr_raw": A_RAW + A_KVT}
        FIRST_D = {"sc_raw": 0, "out_raw": D_SC}

        def a_bank(slot):
            return ps[:, slot % A_BANKS, :]

        def d_bank(slot):
            return ps[:, 4 + slot % D_BANKS, :]

        print('left', nc.sbuf_bytes_remaining)
        block = ctx.enter_context(nc.Block())

        @block.sync
        def _(sp):
            def load_x(b):
                sp.dma_start(x_in[:], x[b]).then_inc(x_loaded, 16)

            def load_residual(b):
                sp.dma_start(x1[:], x[b]).then_inc(res_loaded, 16)

            def body(b, with_next):
                if with_next:
                    sp.wait_ge(lo_ready, 2 * (b + 1))
                    load_x(b + 1)
                for q in range(2):
                    cols = slice(q * HALF, (q + 1) * HALF)
                    sp.wait_ge(pv_free, 4 * b + 2 * (q + 1))
                    sp.dma_start(out[b][:, :, cols], x1[:, :, cols]).then_inc(stored, 16)
                sp.wait_ge(stored, 32 * (b + 1))
                if with_next:
                    load_residual(b + 1)

            sp.dma_start(wqkv_st, wqkv).then_inc(w_loaded, 16)
            load_x(0)
            sp.dma_start(mask_sb[:], masks).then_inc(w_loaded, 16)
            sp.dma_start(dw_sb[:], dw).then_inc(w_loaded, 16)
            sp.dma_start(bn_sb[:], bn).then_inc(w_loaded, 16)
            sp.dma_start(l1b_sb[:], l1b).then_inc(w_loaded, 16)
            sp.dma_start(fg_st, fgw).then_inc(w_loaded, 16)
            sp.dma_start(hw_st, hw).then_inc(w_loaded, 16)
            sp.dma_start(ow_st, ow).then_inc(w_loaded, 16)
            sp.dma_start(pw_sb[:], pw).then_inc(w_loaded, 16)
            sp.dma_start(proj_sb[:], proj).then_inc(w_loaded, 16)
            load_residual(0)
            with sp.Fori(0, B - 1) as b:
                body(b, True)
            body(B - 1, False)

        @block.tensor
        def _(pe):
            def wait_slot(free, count, banks):
                if not isinstance(count, int) or count >= banks:
                    pe.wait_ge(free, count - banks + 1)

            def split_product(dst, terms):
                n = 3 * len(terms)
                k = 0
                for lh, ll, rh, rl in terms:
                    for l, r in ((lh, rh), (lh, rl), (ll, rh)):
                        mm = pe.matmul(dst, l, r, start=(k == 0), stop=(k == n - 1))
                        k += 1
                return mm

            def raw_qkv(b, base, slot):
                for u in range(A_RAW):
                    t, h = u // 2, u % 2
                    if u < 2:
                        pe.wait_ge(lo_ready, 2 * b + h + 1)
                    wait_slot(a_free, base + u, A_BANKS)
                    cols = slice(h * HALF, (h + 1) * HALF)
                    split_product(a_bank(slot + u), [
                        (wqkv_hi[:, k, t * P:(t + 1) * P], wqkv_lo[:, k, t * P:(t + 1) * P],
                         hi[:, k, cols], lo[:, k, cols]) for k in range(CK)]).then_inc(a_full, 1)

            def kv_transposes(b, base, slot, raw_done):
                pe.wait_ge(a_free, raw_done)
                for j in range(A_KVT):
                    wait_slot(a_free, base + j, A_BANKS)
                    n = min(P, IMG - KV0 - j * P)
                    for t in range(CK, TILES):
                        c0 = (t - CK) * P
                        mm = pe.transpose(a_bank(slot + j)[0:n, c0:c0 + P],
                                          raw[:, t, KV0 + j * P:KV0 + j * P + n], ident)
                    mm.then_inc(a_full, 1)

            def scores(base, slot, kv_done, blocks):
                pe.wait_ge(a_free, kv_done)
                wait_slot(d_free, base, D_BANKS)
                dst = d_bank(slot)
                for h in range(CK):
                    for j in range(blocks):
                        mm = pe.matmul(dst[:, h * C:h * C + SCW], kt[:, j, h * P:(h + 1) * P],
                                       vt[:, j, h, 0:SCW], start=(j == 0), stop=(j == blocks - 1))
                mm.then_inc(d_full, 1)

            def outputs(base, slot, q0):
                pe.wait_ge(d_free, base)
                for j in range(D_OUT):
                    wait_slot(d_free, base + j, D_BANKS)
                    dst = d_bank(slot + j)
                    for h in range(CK):
                        mm = pe.matmul(dst[:, h * SDW:(h + 1) * SDW], qp[:, q0 + h, j * P:(j + 1) * P],
                                       sd[:, h, :], start=True, stop=True)
                    mm.then_inc(d_full, 1)

            def out_transposes(base, slot, out_done):
                for u in range(A_TR):
                    t, h = u // 2, u % 2
                    pe.wait_ge(d_free, out_done)
                    wait_slot(a_free, base + u, A_BANKS)
                    for i in range(4):
                        mm = pe.transpose(a_bank(slot + u)[:, i * P:(i + 1) * P],
                                          ot[:, 4 * h + i, t * P:(t + 1) * P], ident)
                    mm.then_inc(a_full, 1)

            def energy(b, i):
                if i >= 2:
                    pe.wait_ge(exp_done, 8 * b + i - 1)
                q = slice(i * P, (i + 1) * P)
                pair = 2 * (i % 2)
                steps = [(f_hi[:, k, q], g) for k in range(CK) for g in (g_hi, g_lo)]
                steps += [(f_lo[:, k, q], g_hi) for k in range(CK)]
                for s, (lhs, g) in enumerate(steps):
                    k = (s // 2) if s < 2 * CK else s - 2 * CK
                    for h in range(2):
                        mm = pe.matmul(ps[:, pair + h, :], lhs, g[:, k, h * HALF:(h + 1) * HALF],
                                       start=(s == 0), stop=(s == len(steps) - 1))
                mm.then_inc(e_full, 1)

            def p_transposes(b, i):
                pe.wait_ge(p_ready, 8 * b + i + 1)
                for u in range(2):
                    if i > 0:
                        pe.wait_ge(t_free, 16 * b + 2 * (i - 1) + u + 1)
                    if i == NB // 2:
                        pe.wait_ge(pv_free, 4 * b + u + 1)
                    for j in range(4):
                        key = (4 * u + j) * P
                        mm = pe.transpose(ps[:, 4 + u, j * P:(j + 1) * P], qp[:, i % 4, key:key + P], ident)
                    mm.then_inc(t_full, 1)

            def values(b, q):
                pe.wait_ge(t_free, 16 * b + 8 * (q + 1))
                for c in range(CK):
                    for j in range(NB):
                        mm = pe.matmul(ps[:, 4 + c, :], ht[:, j, c * P:(c + 1) * P], pt[:, j, :],
                                       start=(j == 0), stop=(j == NB - 1))
                    mm.then_inc(pv_full, 1)

            def body(b, with_next):
                ao, do = a_offsets(with_next), d_offsets(with_next)
                a0, d0 = a_base(b), d_base(b)
                for u in range(A_PWQ):
                    t, h = u // 2, u % 2
                    pe.wait_ge(conv_dve, CONV_STEPS * b + NTAPS * (t + 1))
                    wait_slot(a_free, a0 + u, A_BANKS)
                    pe.matmul(a_bank(u), pw_sb[:, t, :], conv[:, t, h * HALF:(h + 1) * HALF],
                              start=True, stop=True).then_inc(a_full, 1)
                pe.wait_ge(conv_dve, CONV_STEPS * (b + 1))
                for j in range(A_PWKV):
                    u = ao["pwkv"] + j
                    wait_slot(a_free, a0 + u, A_BANKS)
                    for t in range(CK, TILES):
                        c0 = (t - CK) * P
                        mm = pe.matmul(a_bank(u)[:, c0:c0 + P], conv[:, t, j * P:(j + 1) * P], pw_sb[:, t, :],
                                       start=True, stop=True)
                    mm.then_inc(a_full, 1)
                if with_next:
                    raw_qkv(b + 1, a0 + ao["raw"], ao["raw"])
                scores(d0, 0, a0 + ao["pwkv"] + A_PWKV, NB)
                if with_next:
                    kv_transposes(b + 1, a0 + ao["kvt"], ao["kvt"], a0 + ao["kvt"])
                outputs(d0 + do["out_pw"], do["out_pw"], CK)
                if with_next:
                    scores(d0 + do["sc_raw"], do["sc_raw"], a0 + ao["kvt"] + A_KVT, RB)
                out_transposes(a0 + ao["tr_pw"], ao["tr_pw"], d0 + do["out_pw"] + D_OUT)
                if with_next:
                    outputs(d0 + do["out_raw"], do["out_raw"], 0)
                pe.wait_ge(a_free, a0 + ao["tr_pw"] + A_TR)
                for u in range(D_PROJ):
                    c, h = u // 2, u % 2
                    s = do["proj"] + u
                    wait_slot(d_free, d0 + s, D_BANKS)
                    for k in range(2 * CK):
                        mm = pe.matmul(d_bank(s), proj_sb[:, k, c * P:(c + 1) * P],
                                       oc[:, k, h * HALF:(h + 1) * HALF], start=(k == 0), stop=(k == 2 * CK - 1))
                    mm.then_inc(d_full, 1)
                if with_next:
                    out_transposes(a0 + ao["tr_raw"], ao["tr_raw"], d0 + do["out_raw"] + D_OUT)
                pe.wait_ge(d_free, d0 + do["proj"] + D_PROJ)
                for u in range(A_HT):
                    s = ao["ht"] + u
                    wait_slot(a_free, a0 + s, A_BANKS)
                    for i in range(2):
                        n = slice((2 * u + i) * P, (2 * u + i + 1) * P)
                        for k in range(CK):
                            mm = pe.matmul(a_bank(s)[:, i * C:(i + 1) * C], x1[:, k, n], oh_w[:, k, :],
                                           start=(k == 0), stop=(k == CK - 1))
                    mm.then_inc(a_full, 1)
                pe.wait_ge(norm_lo, b + 1)
                for u in range(D_FG):
                    w, c, h = u // 4, (u // 2) % 2, u % 2
                    s = do["fg"] + u
                    wait_slot(d_free, d0 + s, D_BANKS)
                    cols, m = slice(h * HALF, (h + 1) * HALF), slice(c * P, (c + 1) * P)
                    split_product(d_bank(s), [(fg_hi[:, w, k, m], fg_lo[:, w, k, m], hi[:, k, cols], lo[:, k, cols])
                                              for k in range(CK)]).then_inc(d_full, 1)
                pe.wait_ge(a_free, a0 + ao["ht"] + A_HT)
                pe.wait_ge(d_free, d0 + do["fg"] + D_FG)
                for i in range(NB + 2):
                    if i < NB:
                        energy(b, i)
                    if i == NB // 2 + 2:
                        values(b, 0)
                    if i >= 2:
                        p_transposes(b, i - 2)
                values(b, 1)
                if with_next:
                    pe.wait_ge(exp_done, 8 * (b + 1))
                    pe.wait_ge(pv_free, 4 * (b + 1))

            pe.wait_ge(w_loaded, 16 * 10)
            for m in range(CK):
                for k in range(CK):
                    mm = pe.matmul(ps[:, 6, m * C:(m + 1) * C], hw_st[:, k, m * P:(m + 1) * P], ow_st[:, k, :],
                                   start=(k == 0), stop=(k == CK - 1))
            mm.then_inc(prep_pe, 1)
            for m in range(CK):
                for k in range(CK):
                    mm = pe.matmul(ps[:, 7, m:m + 1], ow_st[:, k, m * P:(m + 1) * P], h_b[:, k:k + 1],
                                   start=(k == 0), stop=(k == CK - 1))
            mm.then_inc(prep_pe, 1)
            pe.wait_ge(prep_dve, 2)
            raw_qkv(0, FIRST_A["raw"], 0)
            kv_transposes(0, FIRST_A["kvt"], FIRST_A["kvt"], A_RAW)
            scores(FIRST_D["sc_raw"], 0, A_RAW + A_KVT, RB)
            outputs(FIRST_D["out_raw"], FIRST_D["out_raw"], 0)
            out_transposes(FIRST_A["tr_raw"], FIRST_A["tr_raw"], D_FIRST)
            pe.wait_ge(a_free, A_FIRST)
            with pe.Fori(0, B - 1) as b:
                body(b, True)
            body(B - 1, False)

        @block.scalar
        def _(act):
            def split_x(b):
                act.wait_ge(x_loaded, 16 * (b + 1))
                for h in range(2):
                    cols = slice(h * HALF, (h + 1) * HALF)
                    act.activation(hi[:, :, cols], x_in[:, :, cols], ACT.Copy).then_inc(hi_ready, 1)

            def raw_qkv(base, slot):
                for u in range(A_RAW):
                    t, h = u // 2, u % 2
                    act.wait_ge(a_full, base + u + 1)
                    src = a_bank(slot + u)
                    if t < CK:
                        act.activation(qp[:, t, h * HALF:(h + 1) * HALF], src, ACT.Relu)
                    y0 = PAD + h * SIDE // 2
                    act.copy(raw_img[:, t, y0:y0 + SIDE // 2, PAD:PAD + SIDE],
                             src.rearrange("p (y x) -> p y x", x=SIDE)).then_inc(a_free, 1)

            def keys_values(base, slot, units, used):
                if used is not None:
                    act.wait_ge(d_full, used)
                for j in range(units):
                    act.wait_ge(a_full, base + j + 1)
                    src = a_bank(slot + j)
                    act.activation(kt[:, j, :], src[:, 0:C], ACT.Relu)
                    act.copy(vt[:, j, :, 0:P], src[:, C:2 * C].rearrange("p (h d) -> p h d", h=CK)).then_inc(a_free, 1)

            def out_transposes(base, slot, o0):
                for u in range(A_TR):
                    t, h = u // 2, u % 2
                    act.wait_ge(a_full, base + u + 1)
                    act.copy(oc[:, o0 + t, h * HALF:(h + 1) * HALF], a_bank(slot + u)).then_inc(a_free, 1)

            def body(b, with_next):
                ao, do = a_offsets(with_next), d_offsets(with_next)
                a0, d0 = a_base(b), d_base(b)
                if with_next:
                    split_x(b + 1)
                for u in range(A_PWQ):
                    t, h = u // 2, u % 2
                    act.wait_ge(a_full, a0 + u + 1)
                    act.activation(qp[:, CK + t, h * HALF:(h + 1) * HALF], a_bank(u), ACT.Relu).then_inc(a_free, 1)
                keys_values(a0 + ao["pwkv"], ao["pwkv"], A_PWKV, None)
                act.wait_ge(res_loaded, 16 * (b + 1))
                for k in range(CK):
                    mm = act.activation(x1[:, k, :], x1[:, k, :], ACT.Identity, bias=bn_shift[:, k:k + 1])
                mm.then_inc(res_biased, 1)
                if with_next:
                    raw_qkv(a0 + ao["raw"], ao["raw"])
                    keys_values(a0 + ao["kvt"], ao["kvt"], A_KVT, d0 + do["sc_pw"] + D_SC)
                out_transposes(a0 + ao["tr_pw"], ao["tr_pw"], CK)
                if with_next:
                    act.wait_ge(d_full, d0 + do["proj"] + D_PROJ)
                    out_transposes(a0 + ao["tr_raw"], ao["tr_raw"], 0)
                for u in range(A_HT):
                    s = ao["ht"] + u
                    act.wait_ge(a_full, a0 + s + 1)
                    act.copy(ht[:, 2 * u:2 * u + 2, :],
                             a_bank(s).rearrange("p (i c) -> p i c", i=2)).then_inc(a_free, 1)
                act.wait_ge(norm_ready, b + 1)
                act.activation(hi[:], nf, ACT.Copy).then_inc(norm_hi, 1)
                for u in range(D_FG):
                    w, c, h = u // 4, (u // 2) % 2, u % 2
                    act.wait_ge(d_full, d0 + do["fg"] + u + 1)
                    act.activation((f_hi, g_hi)[w][:, c, h * HALF:(h + 1) * HALF], d_bank(do["fg"] + u),
                                   ACT.Identity, bias=(f_b, g_b)[w][:, c:c + 1]).then_inc(fg_hi_ready, 1)

                def exps(i):
                    act.wait_ge(max_ready, 8 * b + i + 1)
                    if i >= 4:
                        act.wait_ge(t_full, 16 * b + 2 * (i - 4) + 2)
                    pair = 2 * (i % 2)
                    act.activation(qp[:, i % 4, :], ps[:, pair:pair + 2, :].rearrange("p a n -> p (a n)"), ACT.Exp,
                                   bias=neg_max[:, i:i + 1], accum_out=row_sum[:, i:i + 1]).then_inc(exp_done, 1)

                def normalise(i):
                    act.wait_ge(exp_done, 8 * b + i + 1)
                    act.wait_ge(rcp_ready, 8 * b + i + 1)
                    act.mul(qp[:, i % 4, :], qp[:, i % 4, :], row_rcp[:, i:i + 1]).then_inc(p_ready, 1)

                def transposed(i):
                    for u in range(2):
                        act.wait_ge(t_full, 16 * b + 2 * i + u + 1)
                        if i == NB // 2 and u == 0:
                            act.wait_ge(pv_full, 4 * b + 2)
                        q = (i % 4) * P
                        act.copy(pt[:, 4 * u:4 * u + 4, q:q + P],
                                 ps[:, 4 + u, :].rearrange("p (j q) -> p j q", j=4)).then_inc(t_free, 1)

                for i in range(NB + 2):
                    if i < NB:
                        exps(i)
                    if 1 <= i <= NB:
                        normalise(i - 1)
                    if i >= 2:
                        transposed(i - 2)

            act.wait_ge(w_loaded, 160)
            act.activation(wqkv_hi[:], wqkv_st, ACT.Copy).then_inc(prep_act, 1)
            act.activation(fg_hi[:], fg_st, ACT.Copy).then_inc(prep_act, 1)
            split_x(0)
            act.wait_ge(prep_pe, 1)
            act.copy(oh_w[:], ps[:, 6, :].rearrange("p (k m) -> p k m", k=CK)).then_inc(prep_act, 1)
            act.wait_ge(prep_pool, 1)
            raw_qkv(FIRST_A["raw"], 0)
            keys_values(FIRST_A["kvt"], FIRST_A["kvt"], A_KVT, None)
            out_transposes(FIRST_A["tr_raw"], FIRST_A["tr_raw"], 0)
            act.wait_ge(prep_dve, 3)
            with act.Fori(0, B - 1) as b:
                act.wait_ge(conv_dve, CONV_STEPS * (b + 1))
                body(b, True)
            body(B - 1, False)

        @block.vector
        def _(dve):
            def tap(out_ap, t, i, prev, eng):
                dy, dx = divmod(i, TAPS)
                src = raw_img_tap(t, dy, dx)
                w = dw_sb[:, t, i:i + 1]
                if i == 0:
                    return eng.tensor_scalar(out_ap, src, w, None, ALU.mult)
                return eng.scalar_tensor_tensor(out_ap, src, w, prev, ALU.mult, ALU.add)

            def conv_taps(b, r0, c0, first, last):
                for n in range(first, min(last, CONV_STEPS)):
                    t, i = n // NTAPS, n % NTAPS
                    if i == 0:
                        dve.wait_ge(a_free, r0 + 2 * (t + 1))
                    if n > 0:
                        dve.wait_ge(conv_dve, CONV_STEPS * b + n)
                    if i == NTAPS - 1 and c0 is not None:
                        dve.wait_ge(a_full, c0)
                    final = conv[:, t, :].rearrange("p (y x) -> p y x", x=SIDE)
                    tap(final if i == NTAPS - 1 else acc, t, i, acc, dve).then_inc(conv_dve, 1)
                return last

            def split_x(b):
                for h in range(2):
                    dve.wait_ge(hi_ready, 2 * b + h + 1)
                    cols = slice(h * HALF, (h + 1) * HALF)
                    dve.tensor_tensor(lo[:, :, cols], x_in[:, :, cols], hi[:, :, cols].bitcast(F32),
                                      ALU.subtract).then_inc(lo_ready, 1)

            def scores(base, slot):
                dve.wait_ge(d_full, base + 1)
                src = d_bank(slot)
                for h in range(CK):
                    num0, den0 = (HPT, 0) if h == 0 else (0, P)
                    dve.tensor_tensor(sd[:, h, num0:num0 + P], src[:, h * C:h * C + P], mask_blk, ALU.mult)
                    op = dve.tensor_scalar(sd[:, h, den0:den0 + HPT], mask_head, src[:, h * C + P:h * C + P + 1], None,
                                           ALU.mult)
                op.then_inc(d_free, 1)

            def outputs(base, slot, steps, ot_used, taps):
                for j in range(D_OUT):
                    dve.wait_ge(d_full, base + j + 1)
                    if j == 0 and ot_used is not None:
                        dve.wait_ge(a_full, ot_used)
                    src = d_bank(slot + j)
                    dn = den[:, j % 2, :]
                    dve.tensor_scalar(dn.rearrange("p (h g) -> p h g", h=CK),
                                      head_dens(src), ATT_EPS, None, ALU.add).then_inc(dve_step, 1)
                    taps(1)
                    dve.wait_ge(dve_step, steps + 2 * j + 1)
                    dve.reciprocal(dn, dn).then_inc(dve_step, 1)
                    taps(1)
                    dve.wait_ge(dve_step, steps + 2 * j + 2)
                    dve.tensor_tensor(ot[:, j, :].rearrange("p (g d) -> p g d", d=D),
                                      src[:, HPT:HPT + C].rearrange("p (g d) -> p g d", d=D),
                                      dn.unsqueeze(2).to_broadcast([P, CK * HPT, D]), ALU.mult).then_inc(d_free, 1)

            def body(b, with_next):
                ao, do = a_offsets(with_next), d_offsets(with_next)
                a0, d0 = a_base(b), d_base(b)
                s0 = PREP_STEPS + STEPS_OUT + STEPS_BODY * b
                done = [0]

                def taps(n):
                    if with_next:
                        conv_taps(b + 1, a0 + ao["raw"], a0 + ao["raw"], done[0], done[0] + n)
                        done[0] += n

                if with_next:
                    split_x(b + 1)
                taps(6)
                scores(d0, 0)
                taps(6)
                outputs(d0 + do["out_pw"], do["out_pw"], s0, None, lambda n: None)
                if with_next:
                    taps(1)
                    scores(d0 + do["sc_raw"], do["sc_raw"])
                    taps(2)
                    outputs(d0 + do["out_raw"], do["out_raw"], s0 + STEPS_OUT,
                            a0 + ao["tr_pw"] + A_TR, lambda n: None)
                dve.wait_ge(res_biased, b + 1)
                for u in range(D_PROJ):
                    c, h = u // 2, u % 2
                    cols = slice(h * HALF, (h + 1) * HALF)
                    dve.wait_ge(d_full, d0 + do["proj"] + u + 1)
                    dve.scalar_tensor_tensor(x1[:, c, cols], d_bank(do["proj"] + u), bn_scale[:, c:c + 1],
                                             x1[:, c, cols], ALU.mult, ALU.add).then_inc(d_free, 1)
                    taps(1)
                st = s0 + (2 if with_next else 1) * STEPS_OUT
                dve.wait_ge(d_free, d0 + do["proj"] + D_PROJ)
                for c in range(CK):
                    for h in range(2):
                        op = dve.bn_stats(stats[:, c, h, :], x1[:, c, h * HALF:(h + 1) * HALF])
                op.then_inc(dve_step, 1)
                dve.wait_ge(dve_step, st + 1)
                taps(1)
                for c in range(CK):
                    op = dve.bn_aggr(mv[:, c, :], stats[:, c, :, :])
                op.then_inc(dve_step, 1)
                dve.wait_ge(dve_step, st + 2)
                dve.tensor_scalar(stat_ve, mv[:, :, 1], NORM_EPS, None, ALU.add).then_inc(var_ready, 1)
                taps(3)
                dve.wait_ge(rstd_ready, b + 1)
                for c in range(CK):
                    op = dve.tensor_scalar(nf[:, c, :], x1[:, c, :], mv[:, c, 0:1], stat_rstd[:, c:c + 1],
                                           ALU.subtract, ALU.mult)
                op.then_inc(norm_ready, 1)
                taps(1)
                dve.wait_ge(norm_hi, b + 1)
                dve.wait_ge(norm_ready, b + 1)
                dve.tensor_tensor(lo[:], nf, hi[:].bitcast(F32), ALU.subtract).then_inc(norm_lo, 1)
                for u in range(D_FG):
                    w, c, h = u // 4, (u // 2) % 2, u % 2
                    cols = slice(h * HALF, (h + 1) * HALF)
                    dve.wait_ge(fg_hi_ready, 8 * b + u + 1)
                    dve.scalar_tensor_tensor((f_lo, g_lo)[w][:, c, cols], d_bank(do["fg"] + u),
                                             (f_b, g_b)[w][:, c:c + 1], (f_hi, g_hi)[w][:, c, cols].bitcast(F32),
                                             ALU.add, ALU.subtract).then_inc(d_free, 1)

                def final(q):
                    cols = slice(q * HALF, (q + 1) * HALF)
                    for c in range(CK):
                        dve.wait_ge(pv_full, 4 * b + 2 * q + c + 1)
                        dve.scalar_tensor_tensor(x1[:, c, cols], ps[:, 4 + c, :], oh_b[:, c:c + 1], x1[:, c, cols],
                                                 ALU.add, ALU.add).then_inc(pv_free, 1)

                for i in range(NB + 1):
                    if i < NB:
                        dve.wait_ge(e_full, 8 * b + i + 1)
                        pair = 2 * (i % 2)
                        dve.tensor_reduce(neg_max[:, i:i + 1], ps[:, pair:pair + 2, :].rearrange("p a n -> p (a n)"),
                                          AX.X, ALU.max, negate=True).then_inc(max_ready, 1)
                    if i >= 1:
                        dve.wait_ge(exp_done, 8 * b + i)
                        dve.reciprocal(row_rcp[:, i - 1:i], row_sum[:, i - 1:i]).then_inc(rcp_ready, 1)
                        taps(4 if i != NB // 2 + 2 else 6)
                    if i == NB // 2 + 2:
                        final(0)
                taps(CONV_STEPS)
                final(1)

            def raw_img_tap(t, dy, dx):
                o = dy * ROW + dx
                return raw[:, t, o:o + SIDE * ROW].rearrange("p (y x) -> p y x", x=ROW)[:, :, 0:SIDE]

            def head_dens(src):
                groups = src[:, 0:CK * SDW].rearrange("p (c g) -> p c g", g=HPT)
                return groups[:, 0:CK * SDW // HPT:CK * SDW // HPT - 1, :]

            dve.memset(vt[:, :, :, P:SCW + 1], 1.0)
            dve.memset(sd[:], 0.0)
            dve.memset(minus_half, -0.5).then_inc(prep_dve, 1)
            dve.wait_ge(w_loaded, 160)
            dve.wait_ge(prep_act, 2)
            dve.tensor_tensor(wqkv_lo[:], wqkv_st, wqkv_hi[:].bitcast(F32), ALU.subtract)
            dve.tensor_tensor(fg_lo[:], fg_st, fg_hi[:].bitcast(F32), ALU.subtract).then_inc(prep_dve, 1)
            split_x(0)
            dve.tensor_scalar(bn_ve, var, BN_EPS, None, ALU.add).then_inc(dve_step, 1)
            dve.wait_ge(prep_pool, 2)
            dve.tensor_tensor(bn_scale, bn_tmp, gamma, ALU.mult).then_inc(dve_step, 1)
            dve.wait_ge(dve_step, 2)
            dve.tensor_tensor(bn_tmp, bn_scale, mean, ALU.mult).then_inc(dve_step, 1)
            dve.wait_ge(dve_step, 3)
            dve.tensor_tensor(bn_shift, beta, bn_tmp, ALU.subtract).then_inc(prep_dve, 1)
            dve.wait_ge(prep_pe, 2)
            dve.tensor_tensor(oh_b, ps[:, 7, 0:CK], o_b, ALU.add).then_inc(dve_step, 1)
            dve.wait_ge(dve_step, 4)
            dve.wait_ge(prep_act, 3)
            conv_taps(0, 0, None, 0, 40)
            scores(FIRST_D["sc_raw"], 0)
            outputs(FIRST_D["out_raw"], FIRST_D["out_raw"], PREP_STEPS, None, lambda n: None)
            conv_taps(0, 0, None, 40, CONV_STEPS)
            with dve.Fori(0, B - 1) as b:
                body(b, True)
            body(B - 1, False)

        @block.gpsimd
        def _(pool):
            def rstd(b):
                pool.wait_ge(var_ready, b + 1)
                pool.tensor_tensor(stat_rstd, stat_ve, minus_half, ALU.pow).then_inc(rstd_ready, 1)

            pool.memset(raw[:], 0.0).then_inc(prep_pool, 1)
            pool.wait_ge(dve_step, 1)
            pool.tensor_tensor(bn_tmp, bn_ve, minus_half, ALU.pow).then_inc(prep_pool, 1)
            with pool.Fori(0, B - 1) as b:
                rstd(b)
            rstd(B - 1)


def _partitioned(a, rows):
    return np.ascontiguousarray(np.moveaxis(a.reshape(rows, P, *a.shape[1:]), 0, 1))


def kernel(x, L0_conv_wq, L0_conv_wk, L0_conv_wv, L0_conv_dw_kernel, L0_conv_pw_kernel, L0_conv_proj_kernel,
           L0_conv_bn_gamma, L0_conv_bn_beta, L0_conv_bn_mean, L0_conv_bn_var, L1_conv_f_w, L1_conv_f_b,
           L1_conv_g_w, L1_conv_g_b, L1_conv_h_w, L1_conv_h_b, L1_conv_o_w, L1_conv_o_b):
    import concourse.bacc as bacc
    from concourse.bass_utils import run_bass_kernel_spmd

    a = np.asarray
    kind, head, d = np.meshgrid(np.arange(3), np.arange(HEADS), np.arange(D), indexing="ij")
    order = (3 * D * head + D * kind + d).reshape(-1)
    wqkv = np.concatenate([a(L0_conv_wq), a(L0_conv_wk), a(L0_conv_wv)], 0)[order]
    dw = a(L0_conv_dw_kernel).reshape(3 * C, NTAPS)[order]
    pw = a(L0_conv_pw_kernel).reshape(3 * C, D)[order]
    pw_bd = np.zeros((P, TILES, P), pw.dtype)
    for oc_ in range(P):
        g = oc_ // D * D
        pw_bd[g:g + D, :, oc_] = pw.reshape(TILES, P, D)[:, oc_, :].T
    masks = np.concatenate([np.eye(P), np.kron(np.eye(HPT), np.ones((D, D))), np.kron(np.eye(HPT), np.ones((D, 1)))],
                           1).astype(np.float32)
    arrays = {
        "x_dram": np.ascontiguousarray(a(x).reshape(B, CK, P, N).transpose(0, 2, 1, 3)),
        "wqkv_dram": _partitioned(np.ascontiguousarray(wqkv.T), CK),
        "dw_dram": _partitioned(dw, TILES),
        "pw_dram": pw_bd,
        "proj_dram": _partitioned(np.ascontiguousarray(a(L0_conv_proj_kernel).reshape(C, 2 * C).T), 2 * CK),
        "bn_dram": np.ascontiguousarray(np.stack([a(v).reshape(CK, P).T for v in (
            L0_conv_bn_gamma, L0_conv_bn_beta, L0_conv_bn_mean, L0_conv_bn_var)], 1)),
        "fg_dram": np.ascontiguousarray(np.stack([_partitioned(np.ascontiguousarray(a(w).T), CK) for w in (
            L1_conv_f_w, L1_conv_g_w)], 1)),
        "hw_dram": _partitioned(a(L1_conv_h_w), CK),
        "ow_dram": _partitioned(np.ascontiguousarray(a(L1_conv_o_w).T), CK),
        "l1b_dram": np.ascontiguousarray(np.stack([a(v).reshape(CK, P).T for v in (
            L1_conv_f_b, L1_conv_g_b, L1_conv_h_b, L1_conv_o_b)], 1)),
        "masks_dram": masks,
    }
    nc = bacc.Bacc("TRN2", target_bir_lowering=False, num_devices=1)
    ins = [nc.dram_tensor(n, v.shape, mybir.dt.from_np(v.dtype), kind="ExternalInput").ap() for n, v in arrays.items()]
    out = nc.dram_tensor("out_dram", (B, P, CK, N), F32, kind="ExternalOutput").ap()
    x_ap, wqkv_ap, dw_ap, pw_ap, proj_ap, bn_ap, fg_ap, hw_ap, ow_ap, l1b_ap, masks_ap = ins
    conv_seq_kernel(nc, x_ap, wqkv_ap, dw_ap, pw_ap, proj_ap, bn_ap, fg_ap, hw_ap, ow_ap, l1b_ap, masks_ap, out)
    r = run_bass_kernel_spmd(nc, [arrays], core_ids=[0])
    got = r.results[0]["out_dram"]
    return np.ascontiguousarray(got.transpose(0, 2, 1, 3)).reshape(B, C, SIDE, SIDE)
```

```python
from contextlib import ExitStack

import numpy as np
import concourse.bass as bass
from concourse import mybir

ALU = mybir.AluOpType
ACT = mybir.ActivationFunctionType
AX = mybir.AxisListType
F32 = mybir.dt.float32
F32R = mybir.dt.float32r

P = 128
B = 4
C = 256
SIDE = 32
N = SIDE * SIDE
CK = C // P
HALF = N // 2
NB = N // P
D = 8
HEADS = C // D
HPT = P // D
TILES = 3 * CK
TAPS = 5
PAD = TAPS // 2
ROW = SIDE + PAD
IMG = (SIDE + 2 * PAD) * ROW + PAD
IMG += -IMG % 4
KV0 = PAD * ROW
RB = -(-SIDE * ROW // P)
SCW = P + 1
SDW = P + HPT
ROW_BUFS = 3
ATT_EPS = 1e-15
BN_EPS = 1e-5
NORM_EPS = 1e-5
NTAPS = TAPS * TAPS
DVE_TILES = (2, 3, 0, 1)
POOL_TILES = (4, 5)
FUSED_0 = 1
FUSED_1 = 0
FUSED = (FUSED_0, FUSED_1)
FUSED_TAPS = [(t, i) for t in range(CK) for i in range(FUSED[t])]
SHARED_TILE = 1
LATE = 9
LATE_START = FUSED[SHARED_TILE]
SHARED_START = LATE_START + LATE
SHARED_TAPS = 8
KV_TILES = (2, 4, 5, 3)
Q_TILES = (0, 1)
PE_TILE, PE_SHARED_TILE = 5, 0
PE_SHARED_TAPS = 10
PE_TAPS = [(PE_TILE, i) for i in range(NTAPS)] + [
    (PE_SHARED_TILE, FUSED[PE_SHARED_TILE] + i) for i in range(PE_SHARED_TAPS)]
PE_SHARED_END = (PE_SHARED_TILE, FUSED[PE_SHARED_TILE] + PE_SHARED_TAPS)
SHARED_AT = 26
CARRY = 14


def pool_order(taps):
    own = [(t, i) for i in range(NTAPS) for t in POOL_TILES]
    for i in range(SHARED_TAPS):
        own.insert(SHARED_AT + 2 * i, (SHARED_TILE, SHARED_START + i))
    return [tap for tap in own if tap in taps]


LATE_SEQ = [(SHARED_TILE, LATE_START + i) for i in range(LATE)]
ALL_TAPS = [(t, i) for t in range(TILES) for i in range(NTAPS)]
POOL_SEQ = pool_order(ALL_TAPS)
FIRST_POOL_SEQ = pool_order([tap for tap in ALL_TAPS if tap not in PE_TAPS])
DVE_SEQ = [(t, i) for t in DVE_TILES for i in range(NTAPS) if (t, i) not in POOL_SEQ + FUSED_TAPS + LATE_SEQ]
DVE_TAPS, PRODUCTS = len(DVE_SEQ), len(POOL_SEQ)
KV_TAPS = sum(t not in Q_TILES for t, _ in DVE_SEQ)
assert DVE_SEQ.index(PE_SHARED_END) < DVE_TAPS - CARRY
POOL_STARTS = [(t, 0) for t in POOL_TILES] + [(SHARED_TILE, SHARED_START)]
ADD_SEQ = [tap for tap in POOL_SEQ if tap not in POOL_STARTS]
FIRST_ADD_SEQ = [tap for tap in FIRST_POOL_SEQ if tap not in POOL_STARTS]
POOL_ADDS = len(ADD_SEQ)

TAPS_SCORES_PW, TAPS_OUTPUTS_PW, TAPS_SCORES_RAW, TAPS_OUTPUTS_RAW = 10, 6, 2, 2
TAPS_PROJ = (2, 3, 0)
TAPS_STATS = (1, 1)
TAPS_NORM = (2, 3)
TAPS_FG = (0, 1, 1, 1, 1, 2, 0, 1)
TAPS_ATT = (0, 3, 2, 1, 0, 2, 7, 2, 3)
TAPS_FINAL = (8, 6)
PRODUCTS_KVT = (2, 1, 1, 0, 0, 1, 0, 1, 0)
LATES_PWKV = (0, 1, 0, 1, 0, 1, 0, 1)
LATES_RAWKV = (1, 1, 1, 0, 1, 0, 1, 0)
PRODUCTS_PWQ = 4
PRODUCTS_RAWQ = (0, 1, 1, 0)
PRODUCTS_TR = (0, 2, 0, 1)
PRODUCTS_PROJ = 9
PRODUCTS_TR_RAW = (0, 1, 0, 2)
PRODUCTS_HT = (0, 0, 0, 1)
PRODUCTS_FG = (1, 1, 1, 1, 1, 0, 0, 1)
PRODUCTS_ATT = (2, 2, 2, 2, 2, 1, 6, 2, 2, 2)
RSTD_AT = (20, 22)
FIRST_TAPS = 34
FIRST_PRODUCTS_KVT = (0, 0, 0, 0, 1, 0, 0, 0, 1)
FIRST_PRODUCTS_RAWQ = (0, 0, 0, 2)
FIRST_PRODUCTS_CONV = (17, 1, 0)
FIRST_PRODUCTS_TR = (4, 5, 0, 0)

A_BANKS = 4
D_BANKS = 2
A_RAWKV, A_RAWQ, A_KVT, A_PWQ, A_PWKV, A_TR, A_HT = 2 * len(KV_TILES), 2 * len(Q_TILES), RB, 2 * CK, NB, 2 * CK, NB // 2
D_SC, D_OUT, D_PROJ, D_FG = 1, NB, 2 * CK, 4 * CK
A_CONV = 2
A_FIRST = A_RAWKV + A_KVT + A_RAWQ + A_CONV + A_TR + A_CONV
A_BODY = A_RAWKV + A_KVT + A_RAWQ + A_TR + A_PWQ + A_PWKV + A_TR + A_HT
D_FIRST = D_SC + D_OUT
D_BODY = 2 * D_FIRST + D_PROJ + D_FG


def conv_seq_kernel(nc, x, wqkv, dw, pw, proj, bn, fgw, hw, ow, l1b, masks, out):
    with ExitStack() as ctx:
        def sb(name, shape, dt=F32):
            return ctx.enter_context(nc.sbuf_tensor(name, shape, dt))

        def sem(name):
            return ctx.enter_context(nc.semaphore(name))

        fused = sb("fused", [P, len(FUSED_TAPS), P])
        hi = sb("hi", [P, CK, N], F32R)
        lo = sb("lo", [P, CK, N], F32R)
        raw = sb("raw", [P, TILES, IMG])
        conv = sb("conv", [P, TILES, N])
        rows = sb("rows", [P, ROW_BUFS, N])
        late = rows[:, CK, :]
        qp = rows[:, 0:CK, :]
        prod = sb("prod", [P, 2, N])
        kv = sb("kv", [P, RB * C + NB * C])
        vt = sb("vt", [P, RB, CK, SCW + 1])
        sd = sb("sd", [P, CK, SDW])
        oc = sb("oc", [P, 4, N])
        x1 = sb("x1", [P, CK, N])
        f_hi = sb("f_hi", [P, CK, N], F32R)
        f_lo = sb("f_lo", [P, CK, N], F32R)
        g_hi = sb("g_hi", [P, CK, N], F32R)
        g_lo = sb("g_lo", [P, CK, N], F32R)
        wqkv_hi = sb("wqkv_hi", [P, CK, TILES * P], F32R)
        wqkv_lo = sb("wqkv_lo", [P, CK, TILES * P], F32R)
        fg_hi = sb("fg_hi", [P, 2, CK, C], F32R)
        fg_lo = sb("fg_lo", [P, 2, CK, C], F32R)
        pw_sb = sb("pw_sb", [P, TILES, P])
        proj_sb = sb("proj_sb", [P, 2 * CK, C])
        dw_sb = sb("dw_sb", [P, TILES, NTAPS])
        oh_w = sb("oh_w", [P, CK, C])
        mask_sb = sb("mask_sb", [P, 2 * P + HPT])
        bn_sb = sb("bn_sb", [P, 4, CK])
        l1b_sb = sb("l1b_sb", [P, 4, CK])
        small = sb("small", [P, 12, 8])

        ident = mask_sb[:, 0:P]
        mask_blk = mask_sb[:, P:2 * P]
        mask_head = mask_sb[:, 2 * P:2 * P + HPT]
        kt = kv[:, 0:RB * C].rearrange("p (j c) -> p j c", c=C)
        ot = kv[:, RB * C:].rearrange("p (j c) -> p j c", c=C)
        pt = kv[:, 0:NB * HALF].rearrange("p (j q) -> p j q", q=HALF)
        ht = oc[:, 2:4, :].rearrange("p a (j c) -> p (a j) c", c=C)
        nf = x_in = qp
        raw_img = raw[:, :, 0:(SIDE + 2 * PAD) * ROW].rearrange("p t (y x) -> p t y x", x=ROW)
        wqkv_st = conv[:, 0:2, :].rearrange("p a n -> p (a n)")[:, 0:CK * TILES * P].rearrange(
            "p (k m) -> p k m", k=CK)
        fg_st = conv[:, 2, :].rearrange("p (w k m) -> p w k m", w=2, k=CK)
        hw_st = conv[:, 3, 0:CK * C].rearrange("p (k m) -> p k m", k=CK)
        ow_st = conv[:, 3, CK * C:].rearrange("p (k m) -> p k m", k=CK)
        gamma, beta, mean, var = (bn_sb[:, i, :] for i in range(4))
        f_b, g_b, h_b, o_b = (l1b_sb[:, i, :] for i in range(4))
        bn_ve, bn_scale, bn_shift, minus_half, oh_b = (small[:, i, 0:CK] for i in range(5))
        neg_max, row_sum, row_rcp = (small[:, i, :] for i in (5, 6, 7))
        stat_ve, stat_rstd = (small[:, i, 0:CK] for i in (8, 9))
        bn_tmp = small[:, 10, 0:CK]
        stats = sb("stats", [P, CK, 2, 6])
        mv = sb("mv", [P, CK, 2])
        den = sb("den", [P, 2, CK * HPT])

        ps = ctx.enter_context(nc.psum_tensor("ps", [P, 8, 512], F32))
        acc = ps[:, 6:8, :].rearrange("p a n -> p (a n)").rearrange("p (y x) -> p y x", x=SIDE)

        qkv_loaded = sem("qkv_loaded")
        w_loaded = sem("w_loaded")
        x_loaded = sem("x_loaded")
        res_loaded = sem("res_loaded")
        stored = sem("stored")
        weights_hi = sem("weights_hi")
        weights_lo = sem("weights_lo")
        constants_set = sem("constants_set")
        images_cleared = sem("images_cleared")
        bn_ve_ready = sem("bn_ve_ready")
        bn_rstd_ready = sem("bn_rstd_ready")
        bn_ready = sem("bn_ready")
        diagonals_ready = sem("diagonals_ready")
        fused_ready = sem("fused_ready")
        oh_full = sem("oh_full")
        oh_w_ready = sem("oh_w_ready")
        oh_b_ready = sem("oh_b_ready")
        hi_ready = sem("hi_ready")
        lo_ready = sem("lo_ready")
        a_full = sem("a_full")
        a_free = sem("a_free")
        d_full = sem("d_full")
        d_free = sem("d_free")
        conv_dve = sem("conv_dve")
        prod_ready = sem("prod_ready")
        conv_pool = sem("conv_pool")
        dve_step = sem("dve_step")
        res_biased = sem("res_biased")
        var_ready = sem("var_ready")
        rstd_ready = sem("rstd_ready")
        norm_ready = sem("norm_ready")
        norm_hi = sem("norm_hi")
        norm_lo = sem("norm_lo")
        fg_hi_ready = sem("fg_hi_ready")
        e_full = sem("e_full")
        max_ready = sem("max_ready")
        exp_done = sem("exp_done")
        rcp_ready = sem("rcp_ready")
        rows_ready = sem("rows_ready")
        t_full = sem("t_full")
        t_free = sem("t_free")
        pv_full = sem("pv_full")
        pv_free = sem("pv_free")

        W_LOADS = 16 * 9
        STEPS_OUT = 2 * NB
        STEPS_BODY = 2 * STEPS_OUT + 2 * CK
        PREP_STEPS = 2

        def a_base(b):
            return A_FIRST + A_BODY * b

        def d_base(b):
            return D_FIRST + D_BODY * b

        def dve_count(b, n):
            return DVE_TAPS * b + n

        def product_count(b, n):
            return len(FIRST_POOL_SEQ) + (PRODUCTS + LATE) * b - PRODUCTS + n

        def add_count(b, n):
            return len(FIRST_ADD_SEQ) + (POOL_ADDS + LATE - 1) * b - POOL_ADDS + n

        def late_product_count(b, n):
            return product_count(b, PRODUCTS) + n

        def late_add_count(b, n):
            return add_count(b, POOL_ADDS) + n

        def a_offsets(with_next):
            o, at = {}, 0
            for name, n in (("pwkv", A_PWKV), ("raw_kv", A_RAWKV * with_next), ("kvt", A_KVT * with_next),
                            ("pwq", A_PWQ), ("raw_q", A_RAWQ * with_next), ("tr_pw", A_TR), ("tr_raw", A_TR * with_next), ("ht", A_HT)):
                o[name] = at
                at += n
            return o

        def d_offsets(with_next):
            o, at = {}, 0
            for name, n in (("sc_pw", D_SC), ("out_pw", D_OUT), ("sc_raw", D_SC * with_next),
                            ("out_raw", D_OUT * with_next), ("proj", D_PROJ), ("fg", D_FG)):
                o[name] = at
                at += n
            return o

        FIRST_A = {"raw_kv": 0, "kvt": A_RAWKV, "raw_q": A_RAWKV + A_KVT, "conv": A_RAWKV + A_KVT + A_RAWQ,
                   "tr_raw": A_RAWKV + A_KVT + A_RAWQ + A_CONV, "conv_shared": A_FIRST - A_CONV}
        FIRST_D = {"sc_raw": 0, "out_raw": D_SC}

        def a_bank(slot):
            return ps[:, slot % A_BANKS, :]

        def d_bank(slot):
            return ps[:, 4 + slot % D_BANKS, :]

        def tap_view(t, i):
            o = i // TAPS * ROW + i % TAPS
            return raw[:, t, o:o + SIDE * ROW].rearrange("p (y x) -> p y x", x=ROW)[:, :, 0:SIDE]

        def half_tap_view(t, i, h):
            return tap_view(t, i)[:, h * SIDE // 2:(h + 1) * SIDE // 2, :]

        def diagonal(t, i):
            n = PE_TAPS.index((t, i))
            for buffer in (conv[:, PE_SHARED_TILE, :], oc[:, 2, :], oc[:, 3, :], x1[:, 0, :], x1[:, 1, :]):
                if n < N // P:
                    return buffer[:, n * P:(n + 1) * P]
                n -= N // P

        block = ctx.enter_context(nc.Block())

        @block.sync
        def _(sp):
            def load_x(b):
                sp.dma_start(x_in[:], x[b]).then_inc(x_loaded, 16)

            def load_residual(b):
                sp.dma_start(x1[:], x[b]).then_inc(res_loaded, 16)

            def body(b, with_next, with_second):
                for q in range(2):
                    cols = slice(q * HALF, (q + 1) * HALF)
                    sp.wait_ge(pv_free, 4 * b + 2 * (q + 1))
                    sp.dma_start(out[b][:, :, cols], x1[:, :, cols]).then_inc(stored, 16)
                    if q == 0 and with_second:
                        sp.wait_ge(t_full, 16 * (b + 1))
                        load_x(b + 2)
                sp.wait_ge(stored, 32 * (b + 1))
                if with_next:
                    load_residual(b + 1)

            sp.dma_start(wqkv_st, wqkv).then_inc(qkv_loaded, 16)
            load_x(0)
            sp.dma_start(mask_sb[:], masks).then_inc(w_loaded, 16)
            sp.dma_start(dw_sb[:], dw).then_inc(w_loaded, 16)
            sp.dma_start(bn_sb[:], bn).then_inc(w_loaded, 16)
            sp.dma_start(l1b_sb[:], l1b).then_inc(w_loaded, 16)
            sp.dma_start(fg_st, fgw).then_inc(w_loaded, 16)
            sp.dma_start(hw_st, hw).then_inc(w_loaded, 16)
            sp.dma_start(ow_st, ow).then_inc(w_loaded, 16)
            sp.dma_start(pw_sb[:], pw).then_inc(w_loaded, 16)
            sp.dma_start(proj_sb[:], proj).then_inc(w_loaded, 16)
            sp.wait_ge(d_full, D_FIRST)
            load_x(1)
            sp.wait_ge(a_free, A_FIRST)
            load_residual(0)
            with sp.Fori(0, B - 2) as b:
                body(b, True, True)
            body(B - 2, True, False)
            body(B - 1, False, False)

        @block.tensor
        def _(pe):
            def wait_slot(free, count, banks):
                if not isinstance(count, int) or count >= banks:
                    pe.wait_ge(free, count - banks + 1)

            def split_product(dst, terms, before_lo=lambda: None):
                for k, (lh, ll, rh, rl) in enumerate(terms):
                    pe.matmul(dst, lh, rh, start=(k == 0), stop=False)
                    pe.matmul(dst, ll, rh, start=False, stop=False)
                before_lo()
                for k, (lh, ll, rh, rl) in enumerate(terms):
                    mm = pe.matmul(dst, lh, rl, start=False, stop=(k == len(terms) - 1))
                return mm

            def raw_qkv(b, base, slot, tiles):
                for u in range(2 * len(tiles)):
                    t, h = tiles[u // 2], u % 2
                    if u < 2:
                        pe.wait_ge(lo_ready, 2 * b + h + 1)
                    wait_slot(a_free, base + u, A_BANKS)
                    cols = slice(h * HALF, (h + 1) * HALF)
                    split_product(a_bank(slot + u), [
                        (wqkv_hi[:, k, t * P:(t + 1) * P], wqkv_lo[:, k, t * P:(t + 1) * P],
                         hi[:, k, cols], lo[:, k, cols]) for k in range(CK)]).then_inc(a_full, 1)

            def kv_transposes(b, base, slot, raw_done):
                pe.wait_ge(a_free, raw_done)
                for j in range(A_KVT):
                    wait_slot(a_free, base + j, A_BANKS)
                    n = min(P, IMG - KV0 - j * P)
                    for t in range(CK, TILES):
                        c0 = (t - CK) * P
                        mm = pe.transpose(a_bank(slot + j)[0:n, c0:c0 + P],
                                          raw[:, t, KV0 + j * P:KV0 + j * P + n], ident)
                    mm.then_inc(a_full, 1)

            def diagonal_conv(base, slot, t, first, taps):
                for h in range(A_CONV):
                    wait_slot(a_free, base + h, A_BANKS)
                    for i in range(first, first + taps):
                        mm = pe.matmul(a_bank(slot + h).rearrange("p (y x) -> p y x", x=SIDE), diagonal(t, i),
                                       half_tap_view(t, i, h), start=(i == first), stop=(i == first + taps - 1))
                    mm.then_inc(a_full, 1)

            def scores(base, slot, kv_done, blocks):
                pe.wait_ge(a_free, kv_done)
                wait_slot(d_free, base, D_BANKS)
                dst = d_bank(slot)
                for h in range(CK):
                    for j in range(blocks):
                        mm = pe.matmul(dst[:, h * C:h * C + SCW], kt[:, j, h * P:(h + 1) * P],
                                       vt[:, j, h, 0:SCW], start=(j == 0), stop=(j == blocks - 1))
                mm.then_inc(d_full, 1)

            def outputs(base, slot, q_done):
                pe.wait_ge(d_free, base)
                pe.wait_ge(a_free, q_done)
                for j in range(D_OUT):
                    wait_slot(d_free, base + j, D_BANKS)
                    dst = d_bank(slot + j)
                    for h in range(CK):
                        mm = pe.matmul(dst[:, h * SDW:(h + 1) * SDW], qp[:, h, j * P:(j + 1) * P],
                                       sd[:, h, :], start=True, stop=True)
                    mm.then_inc(d_full, 1)

            def out_transposes(base, slot, out_done):
                for u in range(A_TR):
                    t, h = u // 2, u % 2
                    pe.wait_ge(d_free, out_done)
                    wait_slot(a_free, base + u, A_BANKS)
                    for i in range(4):
                        mm = pe.transpose(a_bank(slot + u)[:, i * P:(i + 1) * P],
                                          ot[:, 4 * h + i, t * P:(t + 1) * P], ident)
                    mm.then_inc(a_full, 1)

            def energy(b, i):
                if i >= 2:
                    pe.wait_ge(exp_done, 8 * b + i - 1)
                q = slice(i * P, (i + 1) * P)
                pair = 2 * (i % 2)
                steps = [(f_hi[:, k, q], g) for k in range(CK) for g in (g_hi, g_lo)]
                steps += [(f_lo[:, k, q], g_hi) for k in range(CK)]
                for s, (lhs, g) in enumerate(steps):
                    k = (s // 2) if s < 2 * CK else s - 2 * CK
                    for h in range(2):
                        mm = pe.matmul(ps[:, pair + h, :], lhs, g[:, k, h * HALF:(h + 1) * HALF],
                                       start=(s == 0), stop=(s == len(steps) - 1))
                mm.then_inc(e_full, 1)

            def p_transposes(b, i):
                pe.wait_ge(rows_ready, 8 * b + i + 1)
                for u in range(2):
                    if i > 0:
                        pe.wait_ge(t_free, 16 * b + 2 * (i - 1) + u + 1)
                    if i == NB // 2:
                        pe.wait_ge(pv_free, 4 * b + u + 1)
                    for j in range(4):
                        key = (4 * u + j) * P
                        mm = pe.transpose(ps[:, 4 + u, j * P:(j + 1) * P], rows[:, i % ROW_BUFS, key:key + P], ident)
                    mm.then_inc(t_full, 1)

            def values(b, q):
                pe.wait_ge(t_free, 16 * b + 8 * (q + 1))
                for c in range(CK):
                    for j in range(NB):
                        mm = pe.matmul(ps[:, 4 + c, :], ht[:, j, c * P:(c + 1) * P], pt[:, j, :],
                                       start=(j == 0), stop=(j == NB - 1))
                    mm.then_inc(pv_full, 1)

            def body(b, with_next):
                ao, do = a_offsets(with_next), d_offsets(with_next)
                a0, d0 = a_base(b), d_base(b)
                pe.wait_ge(conv_dve, dve_count(b, KV_TAPS))
                pe.wait_ge(conv_pool, add_count(b, POOL_ADDS))
                for j in range(A_PWKV):
                    u = ao["pwkv"] + j
                    wait_slot(a_free, a0 + u, A_BANKS)
                    for t in range(CK, TILES):
                        c0 = (t - CK) * P
                        mm = pe.matmul(a_bank(u)[:, c0:c0 + P], conv[:, t, j * P:(j + 1) * P], pw_sb[:, t, :],
                                       start=True, stop=True)
                    mm.then_inc(a_full, 1)
                if with_next:
                    raw_qkv(b + 1, a0 + ao["raw_kv"], ao["raw_kv"], KV_TILES)
                scores(d0, 0, a0 + ao["pwkv"] + A_PWKV, NB)
                if with_next:
                    kv_transposes(b + 1, a0 + ao["kvt"], ao["kvt"], a0 + ao["kvt"])
                for i in range(A_PWQ):
                    t, h = i // 2, i % 2
                    u = ao["pwq"] + i
                    wait_slot(a_free, a0 + u, A_BANKS)
                    for tap in range(FUSED[t]):
                        pe.matmul(a_bank(u).rearrange("p (y x) -> p y x", x=SIDE), fused[:, FUSED_TAPS.index((t, tap)), :],
                                  half_tap_view(t, tap, h), start=(tap == 0), stop=False)
                    if i == 0:
                        pe.wait_ge(conv_dve, dve_count(b, DVE_TAPS))
                    mm = pe.matmul(a_bank(u), pw_sb[:, t, :], conv[:, t, h * HALF:(h + 1) * HALF],
                                   start=(FUSED[t] == 0), stop=(t != SHARED_TILE))
                    if t == SHARED_TILE:
                        if h == 0:
                            pe.wait_ge(conv_pool, late_add_count(b, LATE - 1))
                        mm = pe.matmul(a_bank(u), pw_sb[:, t, :], late[:, h * HALF:(h + 1) * HALF],
                                       start=False, stop=True)
                    mm.then_inc(a_full, 1)
                outputs(d0 + do["out_pw"], do["out_pw"], a0 + ao["pwq"] + A_PWQ)
                if with_next:
                    raw_qkv(b + 1, a0 + ao["raw_q"], ao["raw_q"], Q_TILES)
                    scores(d0 + do["sc_raw"], do["sc_raw"], a0 + ao["kvt"] + A_KVT, RB)
                out_transposes(a0 + ao["tr_pw"], ao["tr_pw"], d0 + do["out_pw"] + D_OUT)
                if with_next:
                    outputs(d0 + do["out_raw"], do["out_raw"], a0 + ao["raw_q"] + A_RAWQ)
                pe.wait_ge(a_free, a0 + ao["tr_pw"] + A_TR)
                for u in range(D_PROJ):
                    c, h = u // 2, u % 2
                    s = do["proj"] + u
                    wait_slot(d_free, d0 + s, D_BANKS)
                    for k in range(2 * CK):
                        mm = pe.matmul(d_bank(s), proj_sb[:, k, c * P:(c + 1) * P],
                                       oc[:, k, h * HALF:(h + 1) * HALF], start=(k == 0), stop=(k == 2 * CK - 1))
                    mm.then_inc(d_full, 1)
                if with_next:
                    out_transposes(a0 + ao["tr_raw"], ao["tr_raw"], d0 + do["out_raw"] + D_OUT)
                pe.wait_ge(d_free, d0 + do["proj"] + D_PROJ)
                for u in range(A_HT):
                    s = ao["ht"] + u
                    wait_slot(a_free, a0 + s, A_BANKS)
                    for i in range(2):
                        n = slice((2 * u + i) * P, (2 * u + i + 1) * P)
                        for k in range(CK):
                            mm = pe.matmul(a_bank(s)[:, i * C:(i + 1) * C], x1[:, k, n], oh_w[:, k, :],
                                           start=(k == 0), stop=(k == CK - 1))
                    mm.then_inc(a_full, 1)
                pe.wait_ge(norm_hi, CK * (b + 1))
                for u in range(D_FG):
                    w, c, h = u // 4, (u // 2) % 2, u % 2
                    s = do["fg"] + u
                    wait_slot(d_free, d0 + s, D_BANKS)
                    cols, m = slice(h * HALF, (h + 1) * HALF), slice(c * P, (c + 1) * P)
                    split_product(d_bank(s), [(fg_hi[:, w, k, m], fg_lo[:, w, k, m], hi[:, k, cols], lo[:, k, cols])
                                              for k in range(CK)],
                                  lambda: pe.wait_ge(norm_lo, CK * (b + 1)) if u == 0 else None).then_inc(d_full, 1)
                pe.wait_ge(a_free, a0 + ao["ht"] + A_HT)
                pe.wait_ge(d_free, d0 + do["fg"] + D_FG)
                for i in range(NB + 2):
                    if i < NB:
                        energy(b, i)
                    if i == NB // 2 + 2:
                        values(b, 0)
                    if i >= 2:
                        p_transposes(b, i - 2)
                values(b, 1)
                if with_next:
                    pe.wait_ge(exp_done, 8 * (b + 1))
                    pe.wait_ge(pv_free, 4 * (b + 1))

            pe.wait_ge(weights_lo, 1)
            raw_qkv(0, 0, 0, KV_TILES)
            pe.wait_ge(w_loaded, W_LOADS)
            for m in range(CK):
                for k in range(CK):
                    mm = pe.matmul(ps[:, 4, m * C:(m + 1) * C], hw_st[:, k, m * P:(m + 1) * P], ow_st[:, k, :],
                                   start=(k == 0), stop=(k == CK - 1))
            mm.then_inc(oh_full, 1)
            for m in range(CK):
                for k in range(CK):
                    mm = pe.matmul(ps[:, 5, m:m + 1], ow_st[:, k, m * P:(m + 1) * P], h_b[:, k:k + 1],
                                   start=(k == 0), stop=(k == CK - 1))
            mm.then_inc(oh_full, 1)
            kv_transposes(0, FIRST_A["kvt"], FIRST_A["kvt"], A_RAWKV)
            raw_qkv(0, FIRST_A["raw_q"], FIRST_A["raw_q"], Q_TILES)
            pe.wait_ge(a_free, FIRST_A["raw_q"] + A_RAWQ)
            pe.wait_ge(diagonals_ready, 1)
            diagonal_conv(FIRST_A["conv"], FIRST_A["conv"], PE_TILE, 0, NTAPS)
            pe.wait_ge(oh_w_ready, 1)
            pe.wait_ge(oh_b_ready, 1)
            scores(FIRST_D["sc_raw"], 0, FIRST_A["kvt"] + A_KVT, RB)
            outputs(FIRST_D["out_raw"], FIRST_D["out_raw"], FIRST_A["raw_q"] + A_RAWQ)
            out_transposes(FIRST_A["tr_raw"], FIRST_A["tr_raw"], D_FIRST)
            diagonal_conv(FIRST_A["conv_shared"], FIRST_A["conv_shared"], PE_SHARED_TILE,
                          FUSED[PE_SHARED_TILE], PE_SHARED_TAPS)
            pe.wait_ge(a_free, A_FIRST)
            pe.wait_ge(fused_ready, 1)
            with pe.Fori(0, B - 1) as b:
                body(b, True)
            body(B - 1, False)

        @block.scalar
        def _(act):
            def split_x(b):
                act.wait_ge(x_loaded, 16 * (b + 1))
                for h in range(2):
                    cols = slice(h * HALF, (h + 1) * HALF)
                    act.activation(hi[:, :, cols], x_in[:, :, cols], ACT.Copy).then_inc(hi_ready, 1)

            def raw_qkv(base, slot, tiles, products):
                for u in range(2 * len(tiles)):
                    t, h = tiles[u // 2], u % 2
                    act.wait_ge(a_full, base + u + 1)
                    src = a_bank(slot + u)
                    if t < CK:
                        act.activation(qp[:, t, h * HALF:(h + 1) * HALF], src, ACT.Relu)
                    y0 = PAD + h * SIDE // 2
                    act.copy(raw_img[:, t, y0:y0 + SIDE // 2, PAD:PAD + SIDE],
                             src.rearrange("p (y x) -> p y x", x=SIDE)).then_inc(a_free, 1)
                    products(u)

            def conv_products(b, images, used, first, last):
                batch_0 = isinstance(b, int) and b == 0
                seq, adds = (FIRST_POOL_SEQ, FIRST_ADD_SEQ) if batch_0 else (POOL_SEQ, ADD_SEQ)
                for n in range(first, min(last, len(seq))):
                    t, i = seq[n]
                    if n == 0 or (t, i) == (SHARED_TILE, SHARED_START):
                        act.wait_ge(a_free, images[t in Q_TILES])
                    if (t, i) in POOL_STARTS:
                        if used is not None:
                            act.wait_ge(a_full, used[t in Q_TILES])
                        dst = conv[:, t, :]
                    else:
                        m = adds.index((t, i))
                        if not batch_0:
                            act.wait_ge(conv_pool, add_count(b, max(m - 1, 0)))
                        elif m >= 2:
                            act.wait_ge(conv_pool, m - 1)
                        dst = prod[:, m % 2, :]
                    product(dst, t, i)

            def product(dst, t, i):
                act.activation(dst.rearrange("p (y x) -> p y x", x=SIDE), tap_view(t, i), ACT.Copy,
                               scale=dw_sb[:, t, i:i + 1]).then_inc(prod_ready, 1)

            def late_products(b, first, last):
                for n in range(first, min(last, LATE)):
                    if n > 0:
                        act.wait_ge(conv_pool, late_add_count(b, max(n - 2, 0)))
                    product(late if n == 0 else prod[:, (n - 1) % 2, :], *LATE_SEQ[n])

            def keys_values(base, slot, units, used, products):
                if used is not None:
                    act.wait_ge(d_full, used)
                for j in range(units):
                    act.wait_ge(a_full, base + j + 1)
                    src = a_bank(slot + j)
                    act.activation(kt[:, j, :], src[:, 0:C], ACT.Relu)
                    act.copy(vt[:, j, :, 0:P], src[:, C:2 * C].rearrange("p (h d) -> p h d", h=CK)).then_inc(a_free, 1)
                    products(j)

            def out_transposes(base, slot, o0, products):
                for u in range(A_TR):
                    t, h = u // 2, u % 2
                    act.wait_ge(a_full, base + u + 1)
                    act.copy(oc[:, o0 + t, h * HALF:(h + 1) * HALF], a_bank(slot + u)).then_inc(a_free, 1)
                    products(u)

            def none(u):
                pass

            def diagonal_conv(base, slot, t):
                for h in range(A_CONV):
                    act.wait_ge(a_full, base + h + 1)
                    act.copy(conv[:, t, h * HALF:(h + 1) * HALF], a_bank(slot + h)).then_inc(a_free, 1)

            def body(b, with_next):
                ao, do = a_offsets(with_next), d_offsets(with_next)
                a0, d0 = a_base(b), d_base(b)
                done = [0]

                def products(n):
                    if with_next:
                        conv_products(b + 1, (a0 + ao["kvt"], a0 + ao["raw_q"] + A_RAWQ),
                                      (a0 + ao["raw_kv"], a0 + ao["pwq"] + A_PWQ), done[0], done[0] + n)
                        done[0] += n

                def spread(counts):
                    return lambda u: products(counts[u])

                if with_next:
                    split_x(b + 1)
                late_done = [0]

                def lates(n):
                    late_products(b, late_done[0], late_done[0] + n)
                    late_done[0] += n

                keys_values(a0 + ao["pwkv"], ao["pwkv"], A_PWKV, None, lambda u: lates(LATES_PWKV[u]))
                if with_next:
                    act.wait_ge(conv_dve, dve_count(b, KV_TAPS))
                    act.wait_ge(conv_pool, add_count(b, POOL_ADDS))
                    raw_qkv(a0 + ao["raw_kv"], ao["raw_kv"], KV_TILES, lambda u: lates(LATES_RAWKV[u]))
                lates(LATE)
                if with_next:
                    keys_values(a0 + ao["kvt"], ao["kvt"], A_KVT, d0 + do["sc_pw"] + D_SC, spread(PRODUCTS_KVT))
                if with_next:
                    act.wait_ge(lo_ready, 2 * (b + 2))
                for i in range(A_PWQ):
                    t, h = i // 2, i % 2
                    u = ao["pwq"] + i
                    act.wait_ge(a_full, a0 + u + 1)
                    act.activation(qp[:, t, h * HALF:(h + 1) * HALF], a_bank(u), ACT.Relu).then_inc(a_free, 1)
                act.wait_ge(res_loaded, 16 * (b + 1))
                for k in range(CK):
                    mm = act.activation(x1[:, k, :], x1[:, k, :], ACT.Identity, bias=bn_shift[:, k:k + 1])
                mm.then_inc(res_biased, 1)
                if with_next:
                    products(PRODUCTS_PWQ)
                    act.wait_ge(conv_dve, dve_count(b, DVE_TAPS))
                    act.wait_ge(conv_pool, late_add_count(b, LATE - 1))
                    raw_qkv(a0 + ao["raw_q"], ao["raw_q"], Q_TILES, spread(PRODUCTS_RAWQ))
                out_transposes(a0 + ao["tr_pw"], ao["tr_pw"], CK, spread(PRODUCTS_TR))
                products(PRODUCTS_PROJ)
                if with_next:
                    act.wait_ge(d_full, d0 + do["proj"] + D_PROJ)
                    out_transposes(a0 + ao["tr_raw"], ao["tr_raw"], 0, spread(PRODUCTS_TR_RAW))
                for u in range(A_HT):
                    s = ao["ht"] + u
                    act.wait_ge(a_full, a0 + s + 1)
                    act.copy(ht[:, 2 * u:2 * u + 2, :],
                             a_bank(s).rearrange("p (i c) -> p i c", i=2)).then_inc(a_free, 1)
                    products(PRODUCTS_HT[u])
                for c in range(CK):
                    act.wait_ge(norm_ready, CK * b + c + 1)
                    act.activation(hi[:, c, :], nf[:, c, :], ACT.Copy).then_inc(norm_hi, 1)
                for u in range(D_FG):
                    w, c, h = u // 4, (u // 2) % 2, u % 2
                    act.wait_ge(d_full, d0 + do["fg"] + u + 1)
                    act.activation((f_hi, g_hi)[w][:, c, h * HALF:(h + 1) * HALF], d_bank(do["fg"] + u),
                                   ACT.Identity, bias=(f_b, g_b)[w][:, c:c + 1]).then_inc(fg_hi_ready, 1)
                    products(PRODUCTS_FG[u])

                def exps(i):
                    act.wait_ge(max_ready, 8 * b + i + 1)
                    if i >= ROW_BUFS:
                        act.wait_ge(t_full, 16 * b + 2 * (i - ROW_BUFS) + 2)
                    pair = 2 * (i % 2)
                    act.activation(rows[:, i % ROW_BUFS, :], ps[:, pair:pair + 2, :].rearrange("p a n -> p (a n)"), ACT.Exp,
                                   bias=neg_max[:, i:i + 1], accum_out=row_sum[:, i:i + 1]).then_inc(exp_done, 1)

                def transposed(i):
                    for u in range(2):
                        act.wait_ge(t_full, 16 * b + 2 * i + u + 1)
                        if i == NB // 2 and u == 0:
                            act.wait_ge(pv_full, 4 * b + 2)
                        q = (i % 4) * P
                        act.copy(pt[:, 4 * u:4 * u + 4, q:q + P],
                                 ps[:, 4 + u, :].rearrange("p (j q) -> p j q", j=4)).then_inc(t_free, 1)

                for i in range(NB + 2):
                    if i < NB:
                        exps(i)
                        products(PRODUCTS_ATT[i] - 1)
                    if i >= 2:
                        transposed(i - 2)
                    products(1)
                products(PRODUCTS)

            act.wait_ge(qkv_loaded, 16)
            act.activation(wqkv_hi[:], wqkv_st, ACT.Copy).then_inc(weights_hi, 1)
            split_x(0)
            act.wait_ge(w_loaded, W_LOADS)
            act.activation(fg_hi[:], fg_st, ACT.Copy).then_inc(weights_hi, 1)
            act.wait_ge(images_cleared, 1)
            raw_qkv(0, 0, KV_TILES, none)
            act.wait_ge(lo_ready, 2)
            act.wait_ge(oh_full, 1)
            act.copy(oh_w[:], ps[:, 4, :].rearrange("p (k m) -> p k m", k=CK)).then_inc(oh_w_ready, 1)
            done = [0]

            def products(n):
                conv_products(0, (A_RAWKV, FIRST_A["raw_q"] + A_RAWQ), None, done[0], done[0] + n)
                done[0] += n

            products(1)
            keys_values(FIRST_A["kvt"], FIRST_A["kvt"], A_KVT, None, lambda u: products(FIRST_PRODUCTS_KVT[u]))
            raw_qkv(FIRST_A["raw_q"], FIRST_A["raw_q"], Q_TILES, lambda u: products(FIRST_PRODUCTS_RAWQ[u]))
            products(FIRST_PRODUCTS_CONV[0])
            diagonal_conv(FIRST_A["conv"], FIRST_A["conv"], PE_TILE)
            products(FIRST_PRODUCTS_CONV[1])
            out_transposes(FIRST_A["tr_raw"], FIRST_A["tr_raw"], 0, lambda u: products(FIRST_PRODUCTS_TR[u]))
            products(FIRST_PRODUCTS_CONV[2])
            diagonal_conv(FIRST_A["conv_shared"], FIRST_A["conv_shared"], PE_SHARED_TILE)
            products(PRODUCTS)
            act.wait_ge(bn_ready, 1)
            with act.Fori(0, B - 1) as b:
                body(b, True)
            body(B - 1, False)

        @block.vector
        def _(dve):
            def tap(dst, t, i, before=acc):
                w = dw_sb[:, t, i:i + 1]
                if before is None:
                    return dve.tensor_scalar(dst, tap_view(t, i), w, None, ALU.mult)
                return dve.scalar_tensor_tensor(dst, tap_view(t, i), w, before, ALU.mult, ALU.add)

            def images(kv0, q0):
                return lambda t: (q0 + 2 * (Q_TILES.index(t) + 1) if t in Q_TILES
                                  else kv0 + 2 * (KV_TILES.index(t) + 1))

            def conv_taps(b, made, used, first, last):
                batch_0 = isinstance(b, int) and b == 0
                for n in range(first, last):
                    t, i = DVE_SEQ[n]
                    if batch_0 and (t, i) in PE_TAPS:
                        continue
                    if n == 0 or DVE_SEQ[n - 1][0] != t:
                        dve.wait_ge(a_free, made(t))
                    if n > 0 or not batch_0:
                        skipped = PE_SHARED_TAPS if batch_0 and (t, i) == PE_SHARED_END else 0
                        dve.wait_ge(conv_dve, dve_count(b, n - skipped))
                    if i == NTAPS - 1 and used is not None:
                        dve.wait_ge(a_full, used[t in Q_TILES])
                    final = conv[:, t, :].rearrange("p (y x) -> p y x", x=SIDE)
                    if SHARED_TAPS and t == SHARED_TILE and i == SHARED_START + SHARED_TAPS:
                        adds = FIRST_ADD_SEQ if batch_0 else ADD_SEQ
                        done = adds.index((t, i - 1)) + 1
                        dve.wait_ge(conv_pool, done if batch_0 else add_count(b, POOL_ADDS if last == DVE_TAPS else done))
                        tap(acc, t, i, final).then_inc(conv_dve, 1)
                    elif batch_0 and (t, i) == PE_SHARED_END:
                        dve.wait_ge(a_free, A_FIRST)
                        tap(acc, t, i, final).then_inc(conv_dve, 1 + PE_SHARED_TAPS)
                    else:
                        starts = n == 0 or DVE_SEQ[n - 1][0] != t
                        tap(final if i == NTAPS - 1 else acc, t, i, None if starts else acc).then_inc(conv_dve, 1)

            def split_x(b):
                for h in range(2):
                    dve.wait_ge(hi_ready, 2 * b + h + 1)
                    cols = slice(h * HALF, (h + 1) * HALF)
                    dve.tensor_tensor(lo[:, :, cols], x_in[:, :, cols], hi[:, :, cols].bitcast(F32),
                                      ALU.subtract).then_inc(lo_ready, 1)

            def scores(base, slot):
                dve.wait_ge(d_full, base + 1)
                src = d_bank(slot)
                for h in range(CK):
                    num0, den0 = (HPT, 0) if h == 0 else (0, P)
                    dve.tensor_tensor(sd[:, h, num0:num0 + P], src[:, h * C:h * C + P], mask_blk, ALU.mult)
                    op = dve.tensor_scalar(sd[:, h, den0:den0 + HPT], mask_head, src[:, h * C + P:h * C + P + 1], None,
                                           ALU.mult)
                op.then_inc(d_free, 1)

            def outputs(base, slot, steps, ot_used, taps):
                for j in range(D_OUT):
                    dve.wait_ge(d_full, base + j + 1)
                    if j == 0 and ot_used is not None:
                        dve.wait_ge(a_full, ot_used)
                    src = d_bank(slot + j)
                    dn = den[:, j % 2, :]
                    dve.tensor_scalar(dn.rearrange("p (h g) -> p h g", h=CK),
                                      head_dens(src), ATT_EPS, None, ALU.add).then_inc(dve_step, 1)
                    taps(1)
                    dve.wait_ge(dve_step, steps + 2 * j + 1)
                    dve.reciprocal(dn, dn).then_inc(dve_step, 1)
                    taps(1)
                    dve.wait_ge(dve_step, steps + 2 * j + 2)
                    dve.tensor_tensor(ot[:, j, :].rearrange("p (g d) -> p g d", d=D),
                                      src[:, HPT:HPT + C].rearrange("p (g d) -> p g d", d=D),
                                      dn.unsqueeze(2).to_broadcast([P, CK * HPT, D]), ALU.mult).then_inc(d_free, 1)

            def body(b, with_next):
                ao, do = a_offsets(with_next), d_offsets(with_next)
                a0, d0 = a_base(b), d_base(b)
                s0 = PREP_STEPS + STEPS_OUT + STEPS_BODY * b
                done = [0]

                def taps(n):
                    if with_next:
                        last = min(done[0] + n, DVE_TAPS - CARRY)
                        conv_taps(b + 1, images(a0 + ao["raw_kv"], a0 + ao["raw_q"]),
                                  (a0 + ao["raw_kv"], a0 + ao["pwq"] + A_PWQ), done[0], last)
                        done[0] = last

                if with_next:
                    split_x(b + 1)
                conv_taps(b, lambda t: a0, (a0, a0), DVE_TAPS - CARRY, DVE_TAPS)
                scores(d0, 0)
                taps(TAPS_SCORES_PW)
                outputs(d0 + do["out_pw"], do["out_pw"], s0, None, lambda n: None)
                if with_next:
                    taps(TAPS_OUTPUTS_PW)
                    scores(d0 + do["sc_raw"], do["sc_raw"])
                    taps(TAPS_SCORES_RAW)
                    outputs(d0 + do["out_raw"], do["out_raw"], s0 + STEPS_OUT,
                            a0 + ao["tr_pw"] + A_TR, lambda n: None)
                    taps(TAPS_OUTPUTS_RAW)
                st = s0 + (2 if with_next else 1) * STEPS_OUT
                dve.wait_ge(res_biased, b + 1)

                def statistics(c):
                    dve.wait_ge(d_free, d0 + do["proj"] + 2 * (c + 1))
                    for h in range(2):
                        op = dve.bn_stats(stats[:, c, h, :], x1[:, c, h * HALF:(h + 1) * HALF])
                    op.then_inc(dve_step, 1)
                    dve.wait_ge(dve_step, st + 2 * c + 1)
                    taps(TAPS_STATS[c])
                    dve.bn_aggr(mv[:, c, :], stats[:, c, :, :]).then_inc(dve_step, 1)
                    dve.wait_ge(dve_step, st + 2 * c + 2)
                    dve.tensor_scalar(stat_ve[:, c:c + 1], mv[:, c, 1:2], NORM_EPS, None, ALU.add).then_inc(var_ready, 1)

                def normalise(c):
                    dve.wait_ge(rstd_ready, CK * b + c + 1)
                    dve.tensor_scalar(nf[:, c, :], x1[:, c, :], mv[:, c, 0:1], stat_rstd[:, c:c + 1],
                                      ALU.subtract, ALU.mult).then_inc(norm_ready, 1)

                for u in range(D_PROJ):
                    c, h = u // 2, u % 2
                    cols = slice(h * HALF, (h + 1) * HALF)
                    dve.wait_ge(d_full, d0 + do["proj"] + u + 1)
                    dve.scalar_tensor_tensor(x1[:, c, cols], d_bank(do["proj"] + u), bn_scale[:, c:c + 1],
                                             x1[:, c, cols], ALU.mult, ALU.add).then_inc(d_free, 1)
                    if u != 3:
                        taps(TAPS_PROJ[u])
                    if u == 2:
                        statistics(0)
                statistics(1)
                taps(TAPS_NORM[0])
                normalise(0)
                taps(TAPS_NORM[1])
                normalise(1)
                for c in range(CK):
                    dve.wait_ge(norm_hi, CK * b + c + 1)
                    dve.wait_ge(norm_ready, CK * b + c + 1)
                    dve.tensor_tensor(lo[:, c, :], nf[:, c, :], hi[:, c, :].bitcast(F32),
                                      ALU.subtract).then_inc(norm_lo, 1)
                for u in range(D_FG):
                    w, c, h = u // 4, (u // 2) % 2, u % 2
                    cols = slice(h * HALF, (h + 1) * HALF)
                    dve.wait_ge(fg_hi_ready, 8 * b + u + 1)
                    dve.scalar_tensor_tensor((f_lo, g_lo)[w][:, c, cols], d_bank(do["fg"] + u),
                                             (f_b, g_b)[w][:, c:c + 1], (f_hi, g_hi)[w][:, c, cols].bitcast(F32),
                                             ALU.add, ALU.subtract).then_inc(d_free, 1)
                    taps(TAPS_FG[u])

                def final(q, taps_between):
                    cols = slice(q * HALF, (q + 1) * HALF)
                    for c in range(CK):
                        if c == 1:
                            taps(taps_between)
                        dve.wait_ge(pv_full, 4 * b + 2 * q + c + 1)
                        dve.scalar_tensor_tensor(x1[:, c, cols], ps[:, 4 + c, :], oh_b[:, c:c + 1], x1[:, c, cols],
                                                 ALU.add, ALU.add).then_inc(pv_free, 1)

                for i in range(NB + 1):
                    if i < NB:
                        dve.wait_ge(e_full, 8 * b + i + 1)
                        pair = 2 * (i % 2)
                        dve.tensor_reduce(neg_max[:, i:i + 1], ps[:, pair:pair + 2, :].rearrange("p a n -> p (a n)"),
                                          AX.X, ALU.max, negate=True).then_inc(max_ready, 1)
                    if i >= 1:
                        dve.wait_ge(exp_done, 8 * b + i)
                        dve.reciprocal(row_rcp[:, i - 1:i], row_sum[:, i - 1:i]).then_inc(rcp_ready, 1)
                        dve.wait_ge(rcp_ready, 8 * b + i)
                        row = rows[:, (i - 1) % ROW_BUFS, :]
                        dve.tensor_scalar(row, row, row_rcp[:, i - 1:i], None, ALU.mult).then_inc(rows_ready, 1)
                        taps(TAPS_ATT[i])
                    if i == NB // 2 + 2:
                        final(0, 0)
                taps(TAPS_FINAL[0])
                final(1, TAPS_FINAL[1])
                taps(DVE_TAPS)

            def head_dens(src):
                groups = src[:, 0:CK * SDW].rearrange("p (c g) -> p c g", g=HPT)
                return groups[:, 0:CK * SDW // HPT:CK * SDW // HPT - 1, :]

            dve.memset(vt[:, :, :, P:SCW + 1], 1.0)
            dve.memset(sd[:], 0.0)
            dve.memset(minus_half, -0.5).then_inc(constants_set, 1)
            dve.wait_ge(weights_hi, 1)
            dve.tensor_tensor(wqkv_lo[:], wqkv_st, wqkv_hi[:].bitcast(F32), ALU.subtract).then_inc(weights_lo, 1)
            split_x(0)
            dve.wait_ge(w_loaded, W_LOADS)
            dve.tensor_scalar(bn_ve, var, BN_EPS, None, ALU.add).then_inc(bn_ve_ready, 1)
            dve.wait_ge(weights_lo, 1)
            for t, i in PE_TAPS:
                op = dve.tensor_scalar(diagonal(t, i), ident, dw_sb[:, t, i:i + 1], None, ALU.mult)
            op.then_inc(diagonals_ready, 1)
            conv_taps(0, images(0, FIRST_A["raw_q"]), None, 0, FIRST_TAPS // 2)
            dve.wait_ge(weights_hi, 2)
            dve.tensor_tensor(fg_lo[:], fg_st, fg_hi[:].bitcast(F32), ALU.subtract).then_inc(weights_lo, 1)
            dve.wait_ge(bn_rstd_ready, 1)
            dve.tensor_tensor(bn_scale, bn_tmp, gamma, ALU.mult).then_inc(dve_step, 1)
            dve.wait_ge(dve_step, 1)
            dve.tensor_tensor(bn_tmp, bn_scale, mean, ALU.mult).then_inc(dve_step, 1)
            dve.wait_ge(dve_step, 2)
            dve.tensor_tensor(bn_shift, beta, bn_tmp, ALU.subtract).then_inc(bn_ready, 1)
            dve.wait_ge(oh_full, 2)
            dve.tensor_tensor(oh_b, ps[:, 5, 0:CK], o_b, ALU.add).then_inc(oh_b_ready, 1)
            dve.wait_ge(weights_lo, 2)
            for n, (t, i) in enumerate(FUSED_TAPS):
                op = dve.tensor_scalar(fused[:, n, :], pw_sb[:, t, :], dw_sb[:, t, i:i + 1], None, ALU.mult)
            op.then_inc(fused_ready, 1)
            conv_taps(0, images(0, FIRST_A["raw_q"]), None, FIRST_TAPS // 2, FIRST_TAPS)
            scores(FIRST_D["sc_raw"], 0)
            outputs(FIRST_D["out_raw"], FIRST_D["out_raw"], PREP_STEPS, None, lambda n: None)
            conv_taps(0, images(0, FIRST_A["raw_q"]), None, FIRST_TAPS, DVE_TAPS - CARRY)
            with dve.Fori(0, B - 1) as b:
                body(b, True)
            body(B - 1, False)

        @block.gpsimd
        def _(pool):
            def rstd(b, c):
                pool.wait_ge(var_ready, CK * b + c + 1)
                pool.tensor_tensor(stat_rstd[:, c:c + 1], stat_ve[:, c:c + 1], minus_half[:, c:c + 1],
                                   ALU.pow).then_inc(rstd_ready, 1)

            def conv_adds(b, first, last):
                batch_0 = isinstance(b, int) and b == 0
                seq, adds = (FIRST_POOL_SEQ, FIRST_ADD_SEQ) if batch_0 else (POOL_SEQ, ADD_SEQ)
                for m in range(first, min(last, len(adds))):
                    t, i = adds[m]
                    n = seq.index((t, i)) + 1
                    pool.wait_ge(prod_ready, n if batch_0 else product_count(b, n))
                    if (t, i - 1) in adds:
                        before = adds.index((t, i - 1)) + 1
                        pool.wait_ge(conv_pool, before if batch_0 else add_count(b, before))
                    pool.tensor_tensor(conv[:, t, :], conv[:, t, :], prod[:, m % 2, :], ALU.add).then_inc(conv_pool, 1)

            def late_adds(b):
                for m in range(LATE - 1):
                    pool.wait_ge(prod_ready, late_product_count(b, m + 2))
                    if m > 0:
                        pool.wait_ge(conv_pool, late_add_count(b, m))
                    pool.tensor_tensor(late, late, prod[:, m % 2, :], ALU.add).then_inc(conv_pool, 1)

            pool.memset(raw[:], 0.0).then_inc(images_cleared, 1)
            pool.wait_ge(constants_set, 1)
            pool.wait_ge(bn_ve_ready, 1)
            pool.tensor_tensor(bn_tmp, bn_ve, minus_half, ALU.pow).then_inc(bn_rstd_ready, 1)
            conv_adds(0, 0, POOL_ADDS)
            with pool.Fori(0, B - 1) as b:
                late_adds(b)
                conv_adds(b + 1, 0, RSTD_AT[0])
                rstd(b, 0)
                conv_adds(b + 1, RSTD_AT[0], RSTD_AT[1])
                rstd(b, 1)
                conv_adds(b + 1, RSTD_AT[1], POOL_ADDS)
            late_adds(B - 1)
            rstd(B - 1, 0)
            rstd(B - 1, 1)


def _partitioned(a, rows):
    return np.ascontiguousarray(np.moveaxis(a.reshape(rows, P, *a.shape[1:]), 0, 1))


def kernel(x, L0_conv_wq, L0_conv_wk, L0_conv_wv, L0_conv_dw_kernel, L0_conv_pw_kernel, L0_conv_proj_kernel,
           L0_conv_bn_gamma, L0_conv_bn_beta, L0_conv_bn_mean, L0_conv_bn_var, L1_conv_f_w, L1_conv_f_b,
           L1_conv_g_w, L1_conv_g_b, L1_conv_h_w, L1_conv_h_b, L1_conv_o_w, L1_conv_o_b):
    import concourse.bacc as bacc
    from concourse.bass_utils import run_bass_kernel_spmd

    a = np.asarray
    kind, head, d = np.meshgrid(np.arange(3), np.arange(HEADS), np.arange(D), indexing="ij")
    order = (3 * D * head + D * kind + d).reshape(-1)
    wqkv = np.concatenate([a(L0_conv_wq), a(L0_conv_wk), a(L0_conv_wv)], 0)[order]
    dw = a(L0_conv_dw_kernel).reshape(3 * C, NTAPS)[order]
    pw = a(L0_conv_pw_kernel).reshape(3 * C, D)[order]
    pw_bd = np.zeros((P, TILES, P), pw.dtype)
    for oc_ in range(P):
        g = oc_ // D * D
        pw_bd[g:g + D, :, oc_] = pw.reshape(TILES, P, D)[:, oc_, :].T
    masks = np.concatenate([np.eye(P), np.kron(np.eye(HPT), np.ones((D, D))), np.kron(np.eye(HPT), np.ones((D, 1)))],
                           1).astype(np.float32)
    arrays = {
        "x_dram": np.ascontiguousarray(a(x).reshape(B, CK, P, N).transpose(0, 2, 1, 3)),
        "wqkv_dram": _partitioned(np.ascontiguousarray(wqkv.T), CK),
        "dw_dram": _partitioned(dw, TILES),
        "pw_dram": pw_bd,
        "proj_dram": _partitioned(np.ascontiguousarray(a(L0_conv_proj_kernel).reshape(C, 2 * C).T), 2 * CK),
        "bn_dram": np.ascontiguousarray(np.stack([a(v).reshape(CK, P).T for v in (
            L0_conv_bn_gamma, L0_conv_bn_beta, L0_conv_bn_mean, L0_conv_bn_var)], 1)),
        "fg_dram": np.ascontiguousarray(np.stack([_partitioned(np.ascontiguousarray(a(w).T), CK) for w in (
            L1_conv_f_w, L1_conv_g_w)], 1)),
        "hw_dram": _partitioned(a(L1_conv_h_w), CK),
        "ow_dram": _partitioned(np.ascontiguousarray(a(L1_conv_o_w).T), CK),
        "l1b_dram": np.ascontiguousarray(np.stack([a(v).reshape(CK, P).T for v in (
            L1_conv_f_b, L1_conv_g_b, L1_conv_h_b, L1_conv_o_b)], 1)),
        "masks_dram": masks,
    }
    nc = bacc.Bacc("TRN2", target_bir_lowering=False, num_devices=1)
    ins = [nc.dram_tensor(n, v.shape, mybir.dt.from_np(v.dtype), kind="ExternalInput").ap() for n, v in arrays.items()]
    out = nc.dram_tensor("out_dram", (B, P, CK, N), F32, kind="ExternalOutput").ap()
    x_ap, wqkv_ap, dw_ap, pw_ap, proj_ap, bn_ap, fg_ap, hw_ap, ow_ap, l1b_ap, masks_ap = ins
    conv_seq_kernel(nc, x_ap, wqkv_ap, dw_ap, pw_ap, proj_ap, bn_ap, fg_ap, hw_ap, ow_ap, l1b_ap, masks_ap, out)
    r = run_bass_kernel_spmd(nc, [arrays], core_ids=[0])
    got = r.results[0]["out_dram"]
    return np.ascontiguousarray(got.transpose(0, 2, 1, 3)).reshape(B, C, SIDE, SIDE)
```

```python
from contextlib import ExitStack

import numpy as np
import concourse.bass as bass
from concourse import mybir

ALU = mybir.AluOpType
ACT = mybir.ActivationFunctionType
AX = mybir.AxisListType
F32 = mybir.dt.float32
F32R = mybir.dt.float32r

P = 128
B = 4
C = 256
SIDE = 32
N = SIDE * SIDE
CK = C // P
HALF = N // 2
NB = N // P
D = 8
HEADS = C // D
HPT = P // D
TILES = 3 * CK
TAPS = 5
PAD = TAPS // 2
ROW = SIDE + PAD
IMG = (SIDE + 2 * PAD) * ROW + PAD
IMG += -IMG % 4
KV0 = PAD * ROW
RB = -(-SIDE * ROW // P)
SCW = P + 1
SDW = P + HPT
ROW_BUFS = 3
VALUES_AT = NB // 2 + 2
ATT_EPS = 1e-15
BN_EPS = 1e-5
NORM_EPS = 1e-5
NTAPS = TAPS * TAPS
MIDDLE = NTAPS // 2
TAP_ORDER = [MIDDLE] + [i for i in range(NTAPS) if i not in (MIDDLE, MIDDLE + 1)] + [MIDDLE + 1]
DVE_TILES = (2, 3, 0, 1)
POOL_TILES = (4, 5)
SHARED_TILE = 1
LATE = 10
SHARED_TAPS = 7
PROD_BUFS = 3
KV_TILES = (2, 4, 5, 3)
Q_TILES = (0, 1)
PE_TILE, PE_SHARED_TILE = 5, 0
PE_SHARED_TAPS = 10
PE_TAPS = [(PE_TILE, i) for i in range(NTAPS)] + [(PE_SHARED_TILE, i) for i in range(PE_SHARED_TAPS)]
PE_SHARED_END = (PE_SHARED_TILE, PE_SHARED_TAPS)
SHARED_AT = 32
CARRY = 16


def pool_order(taps):
    own = [(t, i) for i in range(NTAPS) for t in POOL_TILES]
    for i in range(SHARED_TAPS):
        own.insert(SHARED_AT + 2 * i, (SHARED_TILE, LATE + i))
    return [tap for tap in own if tap in taps]


LATE_SEQ = [(SHARED_TILE, i) for i in range(LATE)]
ALL_TAPS = [(t, i) for t in range(TILES) for i in range(NTAPS)]
POOL_SEQ = pool_order(ALL_TAPS)
FIRST_POOL_SEQ = pool_order([tap for tap in ALL_TAPS if tap not in PE_TAPS])
DVE_SEQ = [(t, i) for t in DVE_TILES for i in range(NTAPS) if (t, i) not in POOL_SEQ + LATE_SEQ]
DVE_TAPS, PRODUCTS = len(DVE_SEQ), len(POOL_SEQ)
KV_TAPS = sum(t not in Q_TILES for t, _ in DVE_SEQ)
assert DVE_SEQ.index(PE_SHARED_END) < DVE_TAPS - CARRY
POOL_STARTS = [(t, 0) for t in POOL_TILES] + [(SHARED_TILE, LATE)]
ADD_SEQ = [tap for tap in POOL_SEQ if tap not in POOL_STARTS]
FIRST_ADD_SEQ = [tap for tap in FIRST_POOL_SEQ if tap not in POOL_STARTS]
POOL_ADDS = len(ADD_SEQ)

TAPS_SCORES_PW, TAPS_OUTPUTS_PW, TAPS_SCORES_RAW, TAPS_OUTPUTS_RAW = 10, 7, 0, 2
TAPS_PROJ = (3, 2, 0)
TAPS_STATS = (1, 1)
TAPS_NORM = (2, 1)
TAPS_FG = (0, 0, 1, 1, 2, 1, 1, 1)
TAPS_ATT = (1, 1, 2, 2, 2, 2, 0, 9, 3)
TAPS_FINAL = (9, 8)
PRODUCTS_KVT = (2, 0, 0, 0, 0, 0, 1, 1, 1)
PRODUCTS_RAWKV = (0, 0, 0, 0, 0, 0, 0, 0)
LATES_PWKV = (1, 1, 0, 1, 0, 0, 0, 1)
LATES_RAWKV = (1, 1, 1, 2, 1, 2, 0, 2)
PRODUCTS_PWQ = 5
PRODUCTS_RAWQ = (0, 2, 1, 1)
PRODUCTS_TR = (0, 0, 0, 2)
PRODUCTS_PROJ = 6
PRODUCTS_TR_RAW = (0, 0, 0, 2)
PRODUCTS_HT = (0, 2, 0, 0)
PRODUCTS_FG = (1, 1, 1, 0, 3, 0, 1, 1)
PRODUCTS_ATT = (1, 1, 1, 1, 1, 0, 7, 0)
PRODUCTS_END = (1, 1, 1, 1, 1, 1, 0, 0, 0, 1)
ROWS_ACT = (0, 0, 0, 0, 1, 0, 0, 0)
RSTD_AT = (19, 20)
FIRST_TAPS = 62
FIRST_WEIGHTS = 24
FIRST_PRODUCTS_RAWKV = (0, 0, 0, 0, 2, 0, 1, 1)
FIRST_PRODUCTS_KVT = (0, 0, 0, 0, 0, 0, 0, 0, 0)
FIRST_PRODUCTS_RAWQ = (0, 0, 0, 4)
FIRST_PRODUCTS_CONV = (13, 9, 4)
FIRST_PRODUCTS_TR = (4, 1, 1, 0)

A_BANKS = 4
D_BANKS = 2
A_RAWKV, A_RAWQ, A_KVT, A_PWQ, A_PWKV, A_TR, A_HT = 2 * len(KV_TILES), 2 * len(Q_TILES), RB, 2 * CK, NB, 2 * CK, NB // 2
D_SC, D_OUT, D_PROJ, D_FG = 1, NB, 2 * CK, 4 * CK
A_CONV = 2
A_FIRST = A_RAWKV + A_KVT + A_RAWQ + 2 * A_CONV + A_TR
A_BODY = A_RAWKV + A_KVT + A_RAWQ + A_TR + A_PWQ + A_PWKV + A_TR + A_HT
D_FIRST = D_SC + D_OUT
D_BODY = 2 * D_FIRST + D_PROJ + D_FG


def conv_seq_kernel(nc, x, wqkv, dw, pw, proj, bn, fgw, hw, ow, l1b, masks, out):
    with ExitStack() as ctx:
        def sb(name, shape, dt=F32):
            return ctx.enter_context(nc.sbuf_tensor(name, shape, dt))

        def sem(name):
            return ctx.enter_context(nc.semaphore(name))

        hi = sb("hi", [P, CK, N], F32R)
        lo = sb("lo", [P, CK, N], F32R)
        raw = sb("raw", [P, TILES, IMG])
        conv = sb("conv", [P, TILES, N])
        rows = sb("rows", [P, ROW_BUFS, N])
        late = rows[:, CK, :]
        qp = rows[:, 0:CK, :]
        prod = sb("prod", [P, PROD_BUFS, N])
        kv = sb("kv", [P, RB * C + NB * C])
        vt = sb("vt", [P, RB, CK, SCW + 1])
        sd = sb("sd", [P, CK, SDW])
        oc = sb("oc", [P, 4, N])
        x1 = sb("x1", [P, CK, N])
        f_hi = sb("f_hi", [P, CK, N], F32R)
        f_lo = sb("f_lo", [P, CK, N], F32R)
        g_hi = sb("g_hi", [P, CK, N], F32R)
        g_lo = sb("g_lo", [P, CK, N], F32R)
        wqkv_hi = sb("wqkv_hi", [P, CK, TILES * P], F32R)
        wqkv_lo = sb("wqkv_lo", [P, CK, TILES * P], F32R)
        fg_hi = sb("fg_hi", [P, 2, CK, C], F32R)
        fg_lo = sb("fg_lo", [P, 2, CK, C], F32R)
        pw_sb = sb("pw_sb", [P, TILES, P])
        proj_sb = sb("proj_sb", [P, 2 * CK, C])
        dw_sb = sb("dw_sb", [P, TILES, NTAPS])
        oh_w = sb("oh_w", [P, CK, C])
        mask_sb = sb("mask_sb", [P, 2 * P + HPT])
        bn_sb = sb("bn_sb", [P, 4, CK])
        l1b_sb = sb("l1b_sb", [P, 4, CK])
        small = sb("small", [P, 12, 8])

        ident = mask_sb[:, 0:P]
        mask_blk = mask_sb[:, P:2 * P]
        mask_head = mask_sb[:, 2 * P:2 * P + HPT]
        kt = kv[:, 0:RB * C].rearrange("p (j c) -> p j c", c=C)
        ot = kv[:, RB * C:].rearrange("p (j c) -> p j c", c=C)
        pt = kv[:, 0:NB * HALF].rearrange("p (j q) -> p j q", q=HALF)
        ht = oc[:, 2:4, :].rearrange("p a (j c) -> p (a j) c", c=C)
        nf = x_in = qp
        raw_img = raw[:, :, 0:(SIDE + 2 * PAD) * ROW].rearrange("p t (y x) -> p t y x", x=ROW)
        wqkv_st = conv[:, 0:2, :].rearrange("p a n -> p (a n)")[:, 0:CK * TILES * P].rearrange(
            "p (k m) -> p k m", k=CK)
        fg_st = conv[:, 2, :].rearrange("p (w k m) -> p w k m", w=2, k=CK)
        hw_st = conv[:, 3, 0:CK * C].rearrange("p (k m) -> p k m", k=CK)
        ow_st = conv[:, 3, CK * C:].rearrange("p (k m) -> p k m", k=CK)
        gamma, beta, mean, var = (bn_sb[:, i, :] for i in range(4))
        f_b, g_b, h_b, o_b = (l1b_sb[:, i, :] for i in range(4))
        bn_ve, bn_scale, bn_shift, minus_half, oh_b = (small[:, i, 0:CK] for i in range(5))
        neg_max, row_sum, row_rcp = (small[:, i, :] for i in (5, 6, 7))
        stat_ve, stat_rstd = (small[:, i, 0:CK] for i in (8, 9))
        bn_tmp = small[:, 10, 0:CK]
        stats = sb("stats", [P, CK, 2, 6])
        mv = sb("mv", [P, CK, 2])
        den = sb("den", [P, 2, CK * HPT])

        ps = ctx.enter_context(nc.psum_tensor("ps", [P, 8, 512], F32))
        acc = ps[:, 6:8, :].rearrange("p a n -> p (a n)").rearrange("p (y x) -> p y x", x=SIDE)

        qkv_loaded = sem("qkv_loaded")
        conv_loaded = sem("conv_loaded")
        w_loaded = sem("w_loaded")
        x_loaded = sem("x_loaded")
        res_loaded = sem("res_loaded")
        stored = sem("stored")
        weights_hi = sem("weights_hi")
        weights_lo = sem("weights_lo")
        constants_set = sem("constants_set")
        images_cleared = sem("images_cleared")
        bn_ve_ready = sem("bn_ve_ready")
        bn_rstd_ready = sem("bn_rstd_ready")
        bn_ready = sem("bn_ready")
        diagonals_ready = sem("diagonals_ready")
        oh_full = sem("oh_full")
        oh_w_ready = sem("oh_w_ready")
        hi_ready = sem("hi_ready")
        lo_ready = sem("lo_ready")
        a_full = sem("a_full")
        a_free = sem("a_free")
        d_full = sem("d_full")
        d_free = sem("d_free")
        conv_dve = sem("conv_dve")
        prod_ready = sem("prod_ready")
        conv_pool = sem("conv_pool")
        dve_step = sem("dve_step")
        res_biased = sem("res_biased")
        var_ready = sem("var_ready")
        rstd_ready = sem("rstd_ready")
        norm_ready = sem("norm_ready")
        norm_hi = sem("norm_hi")
        norm_lo = sem("norm_lo")
        fg_hi_ready = sem("fg_hi_ready")
        e_full = sem("e_full")
        max_ready = sem("max_ready")
        exp_done = sem("exp_done")
        rcp_ready = sem("rcp_ready")
        rows_act = sem("rows_act")
        rows_dve = sem("rows_dve")
        t_full = sem("t_full")
        t_free = sem("t_free")
        pv_full = sem("pv_full")
        pv_free = sem("pv_free")

        CONV_LOADS, W_LOADS = 16 * 3, 16 * 6
        STEPS_OUT = 2 * NB
        STEPS_BODY = 2 * STEPS_OUT + 2 * CK
        PREP_STEPS = 2

        def a_base(b):
            return A_FIRST + A_BODY * b

        def pv_count(b, n):
            return 2 * CK * (b + 1) + n

        def d_base(b):
            return D_FIRST + D_BODY * b

        def dve_count(b, n):
            return DVE_TAPS * b + n

        def product_count(b, n):
            return len(FIRST_POOL_SEQ) + (PRODUCTS + LATE) * b - PRODUCTS + n

        def add_count(b, n):
            return len(FIRST_ADD_SEQ) + (POOL_ADDS + LATE - 1) * b - POOL_ADDS + n

        def late_product_count(b, n):
            return product_count(b, PRODUCTS) + n

        def late_add_count(b, n):
            return add_count(b, POOL_ADDS) + n

        def a_offsets(with_next):
            o, at = {}, 0
            for name, n in (("pwkv", A_PWKV), ("raw_kv", A_RAWKV * with_next), ("kvt", A_KVT * with_next),
                            ("pwq", A_PWQ), ("raw_q", A_RAWQ * with_next), ("tr_pw", A_TR),
                            ("tr_raw", A_TR * with_next), ("ht", A_HT)):
                o[name] = at
                at += n
            return o

        def d_offsets(with_next):
            o, at = {}, 0
            for name, n in (("sc_pw", D_SC), ("out_pw", D_OUT), ("sc_raw", D_SC * with_next),
                            ("out_raw", D_OUT * with_next), ("proj", D_PROJ), ("fg", D_FG)):
                o[name] = at
                at += n
            return o

        FIRST_A = {"raw_kv": 0, "kvt": A_RAWKV, "raw_q": A_RAWKV + A_KVT, "conv": A_RAWKV + A_KVT + A_RAWQ,
                   "conv_shared": A_RAWKV + A_KVT + A_RAWQ + A_CONV, "tr_raw": A_FIRST - A_TR}
        FIRST_D = {"sc_raw": 0, "out_raw": D_SC}

        def a_bank(slot):
            return ps[:, slot % A_BANKS, :]

        def d_bank(slot):
            return ps[:, 4 + slot % D_BANKS, :]

        def split_lo(engine, b):
            for h in range(2):
                engine.wait_ge(hi_ready, 2 * b + h + 1)
                cols = slice(h * HALF, (h + 1) * HALF)
                engine.tensor_tensor(lo[:, :, cols], x_in[:, :, cols], hi[:, :, cols].bitcast(F32),
                                     ALU.subtract).then_inc(lo_ready, 1)

        def shift(i):
            return TAP_ORDER[i] // TAPS - PAD, TAP_ORDER[i] % TAPS - PAD

        def weight(t, i):
            return dw_sb[:, t, TAP_ORDER[i]:TAP_ORDER[i] + 1]

        def tap_view(t, i):
            dy, dx = shift(i)
            o = (PAD + dy) * ROW + PAD + dx
            return raw[:, t, o:o + SIDE * ROW].rearrange("p (y x) -> p y x", x=ROW)[:, :, 0:SIDE]

        def rows_count(b, i):
            mine = [k for k in range(NB) if ROWS_ACT[k] == ROWS_ACT[i]]
            return (rows_act if ROWS_ACT[i] else rows_dve), len(mine) * b + mine.index(i) + 1

        def images(kv0, q0):
            return lambda t: (q0 + 2 * (Q_TILES.index(t) + 1) if t in Q_TILES
                              else kv0 + 2 * (KV_TILES.index(t) + 1))

        def inner(image, i):
            dy, dx = shift(i)
            return image[:, max(0, -dy):SIDE - max(0, dy), max(0, -dx):SIDE - max(0, dx)]

        def square(image):
            return image.rearrange("p (y x) -> p y x", x=SIDE)

        def diagonal(t, i):
            n = PE_TAPS.index((t, i))
            for buffer in (conv[:, PE_SHARED_TILE, :], oc[:, 2, :], oc[:, 3, :], x1[:, 0, :], x1[:, 1, :]):
                if n < N // P:
                    return buffer[:, n * P:(n + 1) * P]
                n -= N // P

        block = ctx.enter_context(nc.Block())

        @block.sync
        def _(sp):
            def load_x(b):
                sp.dma_start(x_in[:], x[b]).then_inc(x_loaded, 16)

            def load_residual(b):
                sp.dma_start(x1[:], x[b]).then_inc(res_loaded, 16)

            def body(b, with_next, with_second):
                for q in range(2):
                    cols = slice(q * HALF, (q + 1) * HALF)
                    sp.wait_ge(pv_free, pv_count(b, 2 * (q + 1)))
                    sp.dma_start(out[b][:, :, cols], x1[:, :, cols]).then_inc(stored, 16)
                    if q == 0 and with_second:
                        sp.wait_ge(t_full, 16 * (b + 1))
                        load_x(b + 2)
                sp.wait_ge(stored, 32 * (b + 1))
                if with_next:
                    load_residual(b + 1)

            sp.dma_start(wqkv_st, wqkv).then_inc(qkv_loaded, 16)
            load_x(0)
            sp.dma_start(mask_sb[:], masks).then_inc(conv_loaded, 16)
            sp.dma_start(dw_sb[:], dw).then_inc(conv_loaded, 16)
            sp.dma_start(bn_sb[:], bn).then_inc(conv_loaded, 16)
            sp.dma_start(l1b_sb[:], l1b).then_inc(w_loaded, 16)
            sp.dma_start(fg_st, fgw).then_inc(w_loaded, 16)
            sp.dma_start(hw_st, hw).then_inc(w_loaded, 16)
            sp.dma_start(ow_st, ow).then_inc(w_loaded, 16)
            sp.dma_start(pw_sb[:], pw).then_inc(w_loaded, 16)
            sp.dma_start(proj_sb[:], proj).then_inc(w_loaded, 16)
            sp.wait_ge(d_full, D_FIRST)
            load_x(1)
            sp.wait_ge(a_free, A_FIRST)
            load_residual(0)
            with sp.Fori(0, B - 2) as b:
                body(b, True, True)
            body(B - 2, True, False)
            body(B - 1, False, False)

        @block.tensor
        def _(pe):
            def wait_slot(free, count, banks):
                if not isinstance(count, int) or count >= banks:
                    pe.wait_ge(free, count - banks + 1)

            def split_product(dst, terms, before_lo=lambda: None):
                for k, (lh, ll, rh, rl) in enumerate(terms):
                    pe.matmul(dst, lh, rh, start=(k == 0), stop=False)
                    pe.matmul(dst, ll, rh, start=False, stop=False)
                before_lo()
                for k, (lh, ll, rh, rl) in enumerate(terms):
                    mm = pe.matmul(dst, lh, rl, start=False, stop=(k == len(terms) - 1))
                return mm

            def raw_qkv(b, base, slot, tiles):
                for u in range(2 * len(tiles)):
                    t, h = tiles[u // 2], u % 2
                    if u < 2:
                        pe.wait_ge(lo_ready, 2 * b + h + 1)
                    wait_slot(a_free, base + u, A_BANKS)
                    cols = slice(h * HALF, (h + 1) * HALF)
                    split_product(a_bank(slot + u), [
                        (wqkv_hi[:, k, t * P:(t + 1) * P], wqkv_lo[:, k, t * P:(t + 1) * P],
                         hi[:, k, cols], lo[:, k, cols]) for k in range(CK)]).then_inc(a_full, 1)

            def kv_transposes(b, base, slot, raw_done):
                pe.wait_ge(a_free, raw_done)
                for j in range(A_KVT):
                    wait_slot(a_free, base + j, A_BANKS)
                    n = min(P, IMG - KV0 - j * P)
                    for t in range(CK, TILES):
                        c0 = (t - CK) * P
                        mm = pe.transpose(a_bank(slot + j)[0:n, c0:c0 + P],
                                          raw[:, t, KV0 + j * P:KV0 + j * P + n], ident)
                    mm.then_inc(a_full, 1)

            def diagonal_conv(base, slot, t, taps):
                for h in range(A_CONV):
                    wait_slot(a_free, base + h, A_BANKS)
                    for i in range(taps):
                        dst, view = square(a_bank(slot + h)), tap_view(t, i)
                        y0, y1 = h * SIDE // 2, (h + 1) * SIDE // 2
                        if i > 0:
                            dy, dx = shift(i)
                            y0, y1 = max(y0, -dy), min(y1, SIDE - dy)
                            x0, x_end = max(0, -dx), SIDE - max(0, dx)
                            dst = dst[:, y0 - h * SIDE // 2:y1 - h * SIDE // 2, x0:x_end]
                            view = view[:, y0:y1, x0:x_end]
                        else:
                            view = view[:, y0:y1, :]
                        mm = pe.matmul(dst, diagonal(t, i), view, start=(i == 0), stop=(i == taps - 1))
                    mm.then_inc(a_full, 1)

            def scores(base, slot, kv_done, blocks):
                pe.wait_ge(a_free, kv_done)
                wait_slot(d_free, base, D_BANKS)
                dst = d_bank(slot)
                for h in range(CK):
                    for j in range(blocks):
                        mm = pe.matmul(dst[:, h * C:h * C + SCW], kt[:, j, h * P:(h + 1) * P],
                                       vt[:, j, h, 0:SCW], start=(j == 0), stop=(j == blocks - 1))
                mm.then_inc(d_full, 1)

            def outputs(base, slot, q_done):
                pe.wait_ge(d_free, base)
                pe.wait_ge(a_free, q_done)
                for j in range(D_OUT):
                    wait_slot(d_free, base + j, D_BANKS)
                    dst = d_bank(slot + j)
                    for h in range(CK):
                        mm = pe.matmul(dst[:, h * SDW:(h + 1) * SDW], qp[:, h, j * P:(j + 1) * P],
                                       sd[:, h, :], start=True, stop=True)
                    mm.then_inc(d_full, 1)

            def out_transposes(base, slot, out_done):
                for u in range(A_TR):
                    t, h = u // 2, u % 2
                    pe.wait_ge(d_free, out_done)
                    wait_slot(a_free, base + u, A_BANKS)
                    for i in range(4):
                        mm = pe.transpose(a_bank(slot + u)[:, i * P:(i + 1) * P],
                                          ot[:, 4 * h + i, t * P:(t + 1) * P], ident)
                    mm.then_inc(a_full, 1)

            def energy(b, i):
                if i >= 2:
                    pe.wait_ge(exp_done, 8 * b + i - 1)
                q = slice(i * P, (i + 1) * P)
                pair = 2 * (i % 2)
                steps = [(f_hi[:, k, q], g) for k in range(CK) for g in (g_hi, g_lo)]
                steps += [(f_lo[:, k, q], g_hi) for k in range(CK)]
                for s, (lhs, g) in enumerate(steps):
                    k = (s // 2) if s < 2 * CK else s - 2 * CK
                    for h in range(2):
                        mm = pe.matmul(ps[:, pair + h, :], lhs, g[:, k, h * HALF:(h + 1) * HALF],
                                       start=(s == 0), stop=(s == len(steps) - 1))
                mm.then_inc(e_full, 1)

            def p_transposes(b, i):
                pe.wait_ge(*rows_count(b, i))
                for u in range(2):
                    if i > 0:
                        pe.wait_ge(t_free, 16 * b + 2 * (i - 1) + u + 1)
                    if i == NB // 2:
                        pe.wait_ge(pv_free, pv_count(b, u + 1))
                    for j in range(4):
                        key = (4 * u + j) * P
                        mm = pe.transpose(ps[:, 4 + u, j * P:(j + 1) * P], rows[:, i % ROW_BUFS, key:key + P], ident)
                    mm.then_inc(t_full, 1)

            def values(b, q):
                pe.wait_ge(t_free, 16 * b + 8 * (q + 1))
                for c in range(CK):
                    for j in range(NB):
                        mm = pe.matmul(ps[:, 4 + c, :], ht[:, j, c * P:(c + 1) * P], pt[:, j, :],
                                       start=(j == 0), stop=(j == NB - 1))
                    mm.then_inc(pv_full, 1)

            def body(b, with_next):
                ao, do = a_offsets(with_next), d_offsets(with_next)
                a0, d0 = a_base(b), d_base(b)
                pe.wait_ge(conv_dve, dve_count(b, KV_TAPS))
                pe.wait_ge(conv_pool, add_count(b, POOL_ADDS))
                for j in range(A_PWKV):
                    u = ao["pwkv"] + j
                    wait_slot(a_free, a0 + u, A_BANKS)
                    for t in range(CK, TILES):
                        c0 = (t - CK) * P
                        mm = pe.matmul(a_bank(u)[:, c0:c0 + P], conv[:, t, j * P:(j + 1) * P], pw_sb[:, t, :],
                                       start=True, stop=True)
                    mm.then_inc(a_full, 1)
                if with_next:
                    raw_qkv(b + 1, a0 + ao["raw_kv"], ao["raw_kv"], KV_TILES)
                pe.wait_ge(pv_free, pv_count(b, 0))
                scores(d0, 0, a0 + ao["pwkv"] + A_PWKV, NB)
                if with_next:
                    kv_transposes(b + 1, a0 + ao["kvt"], ao["kvt"], a0 + ao["kvt"])
                for i in range(A_PWQ):
                    t, h = i // 2, i % 2
                    u = ao["pwq"] + i
                    wait_slot(a_free, a0 + u, A_BANKS)
                    if i == 0:
                        pe.wait_ge(conv_dve, dve_count(b, DVE_TAPS))
                    mm = pe.matmul(a_bank(u), pw_sb[:, t, :], conv[:, t, h * HALF:(h + 1) * HALF],
                                   start=True, stop=(t != SHARED_TILE))
                    if t == SHARED_TILE:
                        if h == 0:
                            pe.wait_ge(conv_pool, late_add_count(b, LATE - 1))
                        mm = pe.matmul(a_bank(u), pw_sb[:, t, :], late[:, h * HALF:(h + 1) * HALF],
                                       start=False, stop=True)
                    mm.then_inc(a_full, 1)
                outputs(d0 + do["out_pw"], do["out_pw"], a0 + ao["pwq"] + A_PWQ)
                if with_next:
                    raw_qkv(b + 1, a0 + ao["raw_q"], ao["raw_q"], Q_TILES)
                    scores(d0 + do["sc_raw"], do["sc_raw"], a0 + ao["kvt"] + A_KVT, RB)
                out_transposes(a0 + ao["tr_pw"], ao["tr_pw"], d0 + do["out_pw"] + D_OUT)
                if with_next:
                    outputs(d0 + do["out_raw"], do["out_raw"], a0 + ao["raw_q"] + A_RAWQ)
                pe.wait_ge(a_free, a0 + ao["tr_pw"] + A_TR)
                for u in range(D_PROJ):
                    c, h = u // 2, u % 2
                    s = do["proj"] + u
                    wait_slot(d_free, d0 + s, D_BANKS)
                    for k in range(2 * CK):
                        mm = pe.matmul(d_bank(s), proj_sb[:, k, c * P:(c + 1) * P],
                                       oc[:, k, h * HALF:(h + 1) * HALF], start=(k == 0), stop=(k == 2 * CK - 1))
                    mm.then_inc(d_full, 1)
                if with_next:
                    out_transposes(a0 + ao["tr_raw"], ao["tr_raw"], d0 + do["out_raw"] + D_OUT)
                pe.wait_ge(d_free, d0 + do["proj"] + D_PROJ)
                for u in range(A_HT):
                    s = ao["ht"] + u
                    wait_slot(a_free, a0 + s, A_BANKS)
                    for i in range(2):
                        n = slice((2 * u + i) * P, (2 * u + i + 1) * P)
                        for k in range(CK):
                            mm = pe.matmul(a_bank(s)[:, i * C:(i + 1) * C], x1[:, k, n], oh_w[:, k, :],
                                           start=(k == 0), stop=(k == CK - 1))
                    mm.then_inc(a_full, 1)
                pe.wait_ge(norm_hi, CK * (b + 1))
                for u in range(D_FG):
                    w, c, h = u // 4, (u // 2) % 2, u % 2
                    s = do["fg"] + u
                    wait_slot(d_free, d0 + s, D_BANKS)
                    cols, m = slice(h * HALF, (h + 1) * HALF), slice(c * P, (c + 1) * P)
                    split_product(d_bank(s), [(fg_hi[:, w, k, m], fg_lo[:, w, k, m], hi[:, k, cols], lo[:, k, cols])
                                              for k in range(CK)],
                                  lambda: pe.wait_ge(norm_lo, CK * (b + 1)) if u == 0 else None).then_inc(d_full, 1)
                pe.wait_ge(a_free, a0 + ao["ht"] + A_HT)
                pe.wait_ge(d_free, d0 + do["fg"] + D_FG)
                for i in range(NB + 2):
                    if i < NB and i != VALUES_AT + 1:
                        energy(b, i)
                    if i == VALUES_AT:
                        energy(b, i + 1)
                        values(b, 0)
                    if i >= 2:
                        p_transposes(b, i - 2)
                values(b, 1)
                if with_next:
                    pe.wait_ge(exp_done, 8 * (b + 1))

            pe.wait_ge(weights_lo, 1)
            raw_qkv(0, 0, 0, KV_TILES)
            pe.wait_ge(w_loaded, W_LOADS)
            for m in range(CK):
                for k in range(CK):
                    mm = pe.matmul(ps[:, 4, m * C:(m + 1) * C], hw_st[:, k, m * P:(m + 1) * P], ow_st[:, k, :],
                                   start=(k == 0), stop=(k == CK - 1))
            mm.then_inc(oh_full, 1)
            for m in range(CK):
                for k in range(CK):
                    mm = pe.matmul(ps[:, 5, m:m + 1], ow_st[:, k, m * P:(m + 1) * P], h_b[:, k:k + 1],
                                   start=(k == 0), stop=(k == CK - 1))
            mm.then_inc(oh_full, 1)
            kv_transposes(0, FIRST_A["kvt"], FIRST_A["kvt"], A_RAWKV)
            raw_qkv(0, FIRST_A["raw_q"], FIRST_A["raw_q"], Q_TILES)
            pe.wait_ge(a_free, FIRST_A["raw_q"] + A_RAWQ)
            pe.wait_ge(diagonals_ready, 1)
            diagonal_conv(FIRST_A["conv"], FIRST_A["conv"], PE_TILE, NTAPS)
            diagonal_conv(FIRST_A["conv_shared"], FIRST_A["conv_shared"], PE_SHARED_TILE,
                          PE_SHARED_TAPS)
            pe.wait_ge(oh_w_ready, 1)
            pe.wait_ge(pv_free, pv_count(0, 0))
            scores(FIRST_D["sc_raw"], 0, FIRST_A["kvt"] + A_KVT, RB)
            outputs(FIRST_D["out_raw"], FIRST_D["out_raw"], FIRST_A["raw_q"] + A_RAWQ)
            out_transposes(FIRST_A["tr_raw"], FIRST_A["tr_raw"], D_FIRST)
            pe.wait_ge(a_free, A_FIRST)
            with pe.Fori(0, B - 1) as b:
                body(b, True)
            body(B - 1, False)

        @block.scalar
        def _(act):
            def split_x(b):
                act.wait_ge(x_loaded, 16 * (b + 1))
                for h in range(2):
                    cols = slice(h * HALF, (h + 1) * HALF)
                    act.activation(hi[:, :, cols], x_in[:, :, cols], ACT.Copy).then_inc(hi_ready, 1)

            def raw_qkv(base, slot, tiles, products):
                for u in range(2 * len(tiles)):
                    t, h = tiles[u // 2], u % 2
                    act.wait_ge(a_full, base + u + 1)
                    src = a_bank(slot + u)
                    if t < CK:
                        act.activation(qp[:, t, h * HALF:(h + 1) * HALF], src, ACT.Relu)
                    y0 = PAD + h * SIDE // 2
                    act.copy(raw_img[:, t, y0:y0 + SIDE // 2, PAD:PAD + SIDE],
                             src.rearrange("p (y x) -> p y x", x=SIDE)).then_inc(a_free, 1)
                    products(u)

            def conv_products(b, made, used, first, last):
                batch_0 = isinstance(b, int) and b == 0
                seq, adds = (FIRST_POOL_SEQ, FIRST_ADD_SEQ) if batch_0 else (POOL_SEQ, ADD_SEQ)
                for n in range(first, min(last, len(seq))):
                    t, i = seq[n]
                    if (t, i) in POOL_STARTS:
                        act.wait_ge(a_free, made(t))
                        if used is not None:
                            act.wait_ge(a_full, used[t in Q_TILES])
                        dst, part = conv[:, t, :], False
                    else:
                        m = adds.index((t, i))
                        if not batch_0:
                            act.wait_ge(conv_pool, add_count(b, max(m - PROD_BUFS + 1, 0)))
                        elif m >= PROD_BUFS:
                            act.wait_ge(conv_pool, m - PROD_BUFS + 1)
                        dst, part = prod[:, m % PROD_BUFS, :], True
                    product(dst, t, i, part)

            def product(dst, t, i, part):
                dst, view = square(dst), tap_view(t, i)
                if part:
                    dst, view = inner(dst, i), inner(view, i)
                act.activation(dst, view, ACT.Copy, scale=weight(t, i)).then_inc(prod_ready, 1)

            def late_products(b, first, last):
                for n in range(first, min(last, LATE)):
                    if n > 0:
                        act.wait_ge(conv_pool, late_add_count(b, max(n - PROD_BUFS, 0)))
                    product(late if n == 0 else prod[:, (n - 1) % PROD_BUFS, :], *LATE_SEQ[n], n > 0)

            def keys_values(base, slot, units, used, products):
                if used is not None:
                    act.wait_ge(d_full, used)
                for j in range(units):
                    act.wait_ge(a_full, base + j + 1)
                    src = a_bank(slot + j)
                    act.activation(kt[:, j, :], src[:, 0:C], ACT.Relu)
                    act.copy(vt[:, j, :, 0:P], src[:, C:2 * C].rearrange("p (h d) -> p h d", h=CK)).then_inc(a_free, 1)
                    products(j)

            def out_transposes(base, slot, o0, products):
                for u in range(A_TR):
                    t, h = u // 2, u % 2
                    act.wait_ge(a_full, base + u + 1)
                    act.copy(oc[:, o0 + t, h * HALF:(h + 1) * HALF], a_bank(slot + u)).then_inc(a_free, 1)
                    products(u)

            def diagonal_conv(base, slot, t):
                for h in range(A_CONV):
                    act.wait_ge(a_full, base + h + 1)
                    act.copy(conv[:, t, h * HALF:(h + 1) * HALF], a_bank(slot + h)).then_inc(a_free, 1)

            def body(b, with_next):
                ao, do = a_offsets(with_next), d_offsets(with_next)
                a0, d0 = a_base(b), d_base(b)
                done, late_done = [0], [0]

                def lates(n):
                    late_products(b, late_done[0], late_done[0] + n)
                    late_done[0] += n

                def products(n):
                    if with_next and n:
                        lates(LATE)
                        conv_products(b + 1, images(a0 + ao["raw_kv"], a0 + ao["raw_q"]),
                                      (a0 + ao["raw_kv"], a0 + ao["pwq"] + A_PWQ), done[0], done[0] + n)
                        done[0] += n

                def spread(counts):
                    return lambda u: products(counts[u])

                if with_next:
                    split_x(b + 1)
                keys_values(a0 + ao["pwkv"], ao["pwkv"], A_PWKV, None, lambda u: lates(LATES_PWKV[u]))
                if with_next:
                    act.wait_ge(conv_dve, dve_count(b, KV_TAPS))
                    act.wait_ge(conv_pool, add_count(b, POOL_ADDS))
                    raw_qkv(a0 + ao["raw_kv"], ao["raw_kv"], KV_TILES,
                            lambda u: (lates(LATES_RAWKV[u]), products(PRODUCTS_RAWKV[u])))
                lates(LATE)
                if with_next:
                    keys_values(a0 + ao["kvt"], ao["kvt"], A_KVT, d0 + do["sc_pw"] + D_SC, spread(PRODUCTS_KVT))
                if with_next:
                    act.wait_ge(lo_ready, 2 * (b + 2))
                for i in range(A_PWQ):
                    t, h = i // 2, i % 2
                    u = ao["pwq"] + i
                    act.wait_ge(a_full, a0 + u + 1)
                    act.activation(qp[:, t, h * HALF:(h + 1) * HALF], a_bank(u), ACT.Relu).then_inc(a_free, 1)
                act.wait_ge(res_loaded, 16 * (b + 1))
                for k in range(CK):
                    mm = act.activation(x1[:, k, :], x1[:, k, :], ACT.Identity, bias=bn_shift[:, k:k + 1])
                mm.then_inc(res_biased, 1)
                if with_next:
                    products(PRODUCTS_PWQ)
                    act.wait_ge(conv_dve, dve_count(b, DVE_TAPS))
                    act.wait_ge(conv_pool, late_add_count(b, LATE - 1))
                    raw_qkv(a0 + ao["raw_q"], ao["raw_q"], Q_TILES, spread(PRODUCTS_RAWQ))
                out_transposes(a0 + ao["tr_pw"], ao["tr_pw"], CK, spread(PRODUCTS_TR))
                products(PRODUCTS_PROJ)
                if with_next:
                    act.wait_ge(d_full, d0 + do["proj"] + D_PROJ)
                    out_transposes(a0 + ao["tr_raw"], ao["tr_raw"], 0, spread(PRODUCTS_TR_RAW))
                for u in range(A_HT):
                    s = ao["ht"] + u
                    act.wait_ge(a_full, a0 + s + 1)
                    act.copy(ht[:, 2 * u:2 * u + 2, :],
                             a_bank(s).rearrange("p (i c) -> p i c", i=2)).then_inc(a_free, 1)
                    products(PRODUCTS_HT[u])
                for c in range(CK):
                    act.wait_ge(norm_ready, CK * b + c + 1)
                    act.activation(hi[:, c, :], nf[:, c, :], ACT.Copy).then_inc(norm_hi, 1)
                for u in range(D_FG):
                    w, c, h = u // 4, (u // 2) % 2, u % 2
                    act.wait_ge(d_full, d0 + do["fg"] + u + 1)
                    act.activation((f_hi, g_hi)[w][:, c, h * HALF:(h + 1) * HALF], d_bank(do["fg"] + u),
                                   ACT.Identity, bias=(f_b, g_b)[w][:, c:c + 1]).then_inc(fg_hi_ready, 1)
                    products(PRODUCTS_FG[u])

                def exps(i):
                    act.wait_ge(max_ready, 8 * b + i + 1)
                    if i >= ROW_BUFS:
                        act.wait_ge(t_full, 16 * b + 2 * (i - ROW_BUFS) + 2)
                    pair = 2 * (i % 2)
                    act.activation(rows[:, i % ROW_BUFS, :], ps[:, pair:pair + 2, :].rearrange("p a n -> p (a n)"), ACT.Exp,
                                   bias=neg_max[:, i:i + 1], accum_out=row_sum[:, i:i + 1]).then_inc(exp_done, 1)

                def normalise(i):
                    act.wait_ge(exp_done, 8 * b + i + 1)
                    act.wait_ge(rcp_ready, 8 * b + i + 1)
                    row = rows[:, i % ROW_BUFS, :]
                    act.mul(row, row, row_rcp[:, i:i + 1]).then_inc(rows_act, 1)

                def transposed(i):
                    for u in range(2):
                        act.wait_ge(t_full, 16 * b + 2 * i + u + 1)
                        if i == NB // 2 and u == 0:
                            act.wait_ge(pv_full, 4 * b + 2)
                        q = (i % 4) * P
                        act.copy(pt[:, 4 * u:4 * u + 4, q:q + P],
                                 ps[:, 4 + u, :].rearrange("p (j q) -> p j q", j=4)).then_inc(t_free, 1)

                for i in range(NB + 2):
                    if i < NB:
                        exps(i)
                        products(PRODUCTS_ATT[i])
                    if 1 <= i <= NB and ROWS_ACT[i - 1]:
                        normalise(i - 1)
                    if i >= 2:
                        transposed(i - 2)
                    products(PRODUCTS_END[i])
                products(PRODUCTS)

            act.wait_ge(qkv_loaded, 16)
            act.activation(wqkv_hi[:], wqkv_st, ACT.Copy).then_inc(weights_hi, 1)
            split_x(0)
            done = [0]

            def products(n):
                conv_products(0, images(0, FIRST_A["raw_q"]), None, done[0], done[0] + n)
                done[0] += n

            act.wait_ge(conv_loaded, CONV_LOADS)
            act.wait_ge(images_cleared, 1)
            raw_qkv(0, 0, KV_TILES, lambda u: products(FIRST_PRODUCTS_RAWKV[u]))
            act.wait_ge(w_loaded, W_LOADS)
            act.activation(fg_hi[:], fg_st, ACT.Copy).then_inc(weights_hi, 1)
            act.wait_ge(lo_ready, 2)
            act.wait_ge(oh_full, 1)
            act.copy(oh_w[:], ps[:, 4, :].rearrange("p (k m) -> p k m", k=CK)).then_inc(oh_w_ready, 1)
            keys_values(FIRST_A["kvt"], FIRST_A["kvt"], A_KVT, None, lambda u: products(FIRST_PRODUCTS_KVT[u]))
            raw_qkv(FIRST_A["raw_q"], FIRST_A["raw_q"], Q_TILES, lambda u: products(FIRST_PRODUCTS_RAWQ[u]))
            products(FIRST_PRODUCTS_CONV[0])
            diagonal_conv(FIRST_A["conv"], FIRST_A["conv"], PE_TILE)
            products(FIRST_PRODUCTS_CONV[1])
            diagonal_conv(FIRST_A["conv_shared"], FIRST_A["conv_shared"], PE_SHARED_TILE)
            products(FIRST_PRODUCTS_CONV[2])
            out_transposes(FIRST_A["tr_raw"], FIRST_A["tr_raw"], 0, lambda u: products(FIRST_PRODUCTS_TR[u]))
            products(PRODUCTS)
            act.wait_ge(bn_ready, 1)
            with act.Fori(0, B - 1) as b:
                body(b, True)
            body(B - 1, False)

        @block.vector
        def _(dve):
            def tap(dst, t, i, before=acc):
                w = weight(t, i)
                if before is None:
                    return dve.tensor_scalar(dst, tap_view(t, i), w, None, ALU.mult)
                view = tap_view(t, i)
                if dst is before:
                    view, dst, before = (inner(a, i) for a in (view, dst, before))
                return dve.scalar_tensor_tensor(dst, view, w, before, ALU.mult, ALU.add)

            def conv_taps(b, made, used, first, last):
                batch_0 = isinstance(b, int) and b == 0
                for n in range(first, last):
                    t, i = DVE_SEQ[n]
                    if batch_0 and (t, i) in PE_TAPS:
                        continue
                    if n == 0 or DVE_SEQ[n - 1][0] != t:
                        dve.wait_ge(a_free, made(t))
                    if n > 0 or not batch_0:
                        skipped = PE_SHARED_TAPS if batch_0 and (t, i) == PE_SHARED_END else 0
                        dve.wait_ge(conv_dve, dve_count(b, n - skipped))
                    if i == NTAPS - 1 and used is not None:
                        dve.wait_ge(a_full, used[t in Q_TILES])
                    final = square(conv[:, t, :])
                    if SHARED_TAPS and t == SHARED_TILE and i == LATE + SHARED_TAPS:
                        adds = FIRST_ADD_SEQ if batch_0 else ADD_SEQ
                        done = adds.index((t, i - 1)) + 1
                        if last == DVE_TAPS:
                            done = POOL_ADDS
                        dve.wait_ge(conv_pool, done if batch_0 else add_count(b, done))
                        tap(acc, t, i, final).then_inc(conv_dve, 1)
                    elif batch_0 and (t, i) == PE_SHARED_END:
                        dve.wait_ge(a_free, FIRST_A["conv_shared"] + A_CONV)
                        tap(acc, t, i, final).then_inc(conv_dve, 1 + PE_SHARED_TAPS)
                    else:
                        starts = n == 0 or DVE_SEQ[n - 1][0] != t
                        tap(final if i == NTAPS - 1 else acc, t, i, None if starts else acc).then_inc(conv_dve, 1)

            def scores(base, slot):
                dve.wait_ge(d_full, base + 1)
                src = d_bank(slot)
                for h in range(CK):
                    num0, den0 = (HPT, 0) if h == 0 else (0, P)
                    dve.tensor_tensor(sd[:, h, num0:num0 + P], src[:, h * C:h * C + P], mask_blk, ALU.mult)
                    op = dve.tensor_scalar(sd[:, h, den0:den0 + HPT], mask_head, src[:, h * C + P:h * C + P + 1], None,
                                           ALU.mult)
                op.then_inc(d_free, 1)

            def outputs(base, slot, steps, ot_used):
                for j in range(D_OUT):
                    dve.wait_ge(d_full, base + j + 1)
                    if j == 0 and ot_used is not None:
                        dve.wait_ge(a_full, ot_used)
                    src = d_bank(slot + j)
                    dn = den[:, j % 2, :]
                    dve.tensor_scalar(dn.rearrange("p (h g) -> p h g", h=CK),
                                      head_dens(src), ATT_EPS, None, ALU.add).then_inc(dve_step, 1)
                    dve.wait_ge(dve_step, steps + 2 * j + 1)
                    dve.reciprocal(dn, dn).then_inc(dve_step, 1)
                    dve.wait_ge(dve_step, steps + 2 * j + 2)
                    dve.tensor_tensor(ot[:, j, :].rearrange("p (g d) -> p g d", d=D),
                                      src[:, HPT:HPT + C].rearrange("p (g d) -> p g d", d=D),
                                      dn.unsqueeze(2).to_broadcast([P, CK * HPT, D]), ALU.mult).then_inc(d_free, 1)

            def body(b, with_next):
                ao, do = a_offsets(with_next), d_offsets(with_next)
                a0, d0 = a_base(b), d_base(b)
                s0 = PREP_STEPS + STEPS_OUT + STEPS_BODY * b
                done = [0]

                def taps(n):
                    if with_next:
                        last = min(done[0] + n, DVE_TAPS - CARRY)
                        conv_taps(b + 1, images(a0 + ao["raw_kv"], a0 + ao["raw_q"]),
                                  (a0 + ao["raw_kv"], a0 + ao["pwq"] + A_PWQ), done[0], last)
                        done[0] = last

                conv_taps(b, lambda t: a0, (a0, a0), DVE_TAPS - CARRY, DVE_TAPS)
                scores(d0, 0)
                taps(TAPS_SCORES_PW)
                outputs(d0 + do["out_pw"], do["out_pw"], s0, None)
                if with_next:
                    taps(TAPS_OUTPUTS_PW)
                    scores(d0 + do["sc_raw"], do["sc_raw"])
                    taps(TAPS_SCORES_RAW)
                    outputs(d0 + do["out_raw"], do["out_raw"], s0 + STEPS_OUT,
                            a0 + ao["tr_pw"] + A_TR)
                    taps(TAPS_OUTPUTS_RAW)
                st = s0 + (2 if with_next else 1) * STEPS_OUT
                dve.wait_ge(res_biased, b + 1)

                def statistics(c):
                    dve.wait_ge(d_free, d0 + do["proj"] + 2 * (c + 1))
                    for h in range(2):
                        op = dve.bn_stats(stats[:, c, h, :], x1[:, c, h * HALF:(h + 1) * HALF])
                    op.then_inc(dve_step, 1)
                    dve.wait_ge(dve_step, st + 2 * c + 1)
                    taps(TAPS_STATS[c])
                    dve.bn_aggr(mv[:, c, :], stats[:, c, :, :]).then_inc(dve_step, 1)
                    dve.wait_ge(dve_step, st + 2 * c + 2)
                    dve.tensor_scalar(stat_ve[:, c:c + 1], mv[:, c, 1:2], NORM_EPS, None, ALU.add).then_inc(var_ready, 1)

                def normalise(c):
                    dve.wait_ge(rstd_ready, CK * b + c + 1)
                    dve.tensor_scalar(nf[:, c, :], x1[:, c, :], mv[:, c, 0:1], stat_rstd[:, c:c + 1],
                                      ALU.subtract, ALU.mult).then_inc(norm_ready, 1)

                for u in range(D_PROJ):
                    c, h = u // 2, u % 2
                    cols = slice(h * HALF, (h + 1) * HALF)
                    dve.wait_ge(d_full, d0 + do["proj"] + u + 1)
                    dve.scalar_tensor_tensor(x1[:, c, cols], d_bank(do["proj"] + u), bn_scale[:, c:c + 1],
                                             x1[:, c, cols], ALU.mult, ALU.add).then_inc(d_free, 1)
                    if u != 3:
                        taps(TAPS_PROJ[u])
                    if u == 2:
                        statistics(0)
                statistics(1)
                taps(TAPS_NORM[0])
                normalise(0)
                taps(TAPS_NORM[1])
                normalise(1)
                for c in range(CK):
                    dve.wait_ge(norm_hi, CK * b + c + 1)
                    dve.wait_ge(norm_ready, CK * b + c + 1)
                    dve.tensor_tensor(lo[:, c, :], nf[:, c, :], hi[:, c, :].bitcast(F32),
                                      ALU.subtract).then_inc(norm_lo, 1)
                for u in range(D_FG):
                    w, c, h = u // 4, (u // 2) % 2, u % 2
                    cols = slice(h * HALF, (h + 1) * HALF)
                    dve.wait_ge(fg_hi_ready, 8 * b + u + 1)
                    dve.scalar_tensor_tensor((f_lo, g_lo)[w][:, c, cols], d_bank(do["fg"] + u),
                                             (f_b, g_b)[w][:, c:c + 1], (f_hi, g_hi)[w][:, c, cols].bitcast(F32),
                                             ALU.add, ALU.subtract).then_inc(d_free, 1)
                    taps(TAPS_FG[u])

                def final(q, taps_between):
                    cols = slice(q * HALF, (q + 1) * HALF)
                    for c in range(CK):
                        if c == 1:
                            taps(taps_between)
                        dve.wait_ge(pv_full, 4 * b + 2 * q + c + 1)
                        dve.scalar_tensor_tensor(x1[:, c, cols], ps[:, 4 + c, :], oh_b[:, c:c + 1], x1[:, c, cols],
                                                 ALU.add, ALU.add).then_inc(pv_free, 1)

                for i in range(NB + 1):
                    if i < NB:
                        dve.wait_ge(e_full, 8 * b + i + 1)
                        pair = 2 * (i % 2)
                        dve.tensor_reduce(neg_max[:, i:i + 1], ps[:, pair:pair + 2, :].rearrange("p a n -> p (a n)"),
                                          AX.X, ALU.max, negate=True).then_inc(max_ready, 1)
                    if i >= 1:
                        dve.wait_ge(exp_done, 8 * b + i)
                        dve.reciprocal(row_rcp[:, i - 1:i], row_sum[:, i - 1:i]).then_inc(rcp_ready, 1)
                        if not ROWS_ACT[i - 1]:
                            dve.wait_ge(rcp_ready, 8 * b + i)
                            row = rows[:, (i - 1) % ROW_BUFS, :]
                            dve.tensor_scalar(row, row, row_rcp[:, i - 1:i], None, ALU.mult).then_inc(rows_dve, 1)
                        taps(TAPS_ATT[i])
                    if i == VALUES_AT + 1:
                        final(0, 0)
                taps(TAPS_FINAL[0])
                final(1, TAPS_FINAL[1])
                taps(DVE_TAPS)

            def head_dens(src):
                groups = src[:, 0:CK * SDW].rearrange("p (c g) -> p c g", g=HPT)
                return groups[:, 0:CK * SDW // HPT:CK * SDW // HPT - 1, :]

            dve.memset(vt[:, :, :, P:SCW + 1], 1.0)
            dve.memset(sd[:], 0.0)
            dve.memset(minus_half, -0.5).then_inc(constants_set, 1)
            dve.wait_ge(weights_hi, 1)
            dve.tensor_tensor(wqkv_lo[:], wqkv_st, wqkv_hi[:].bitcast(F32), ALU.subtract).then_inc(weights_lo, 1)
            split_lo(dve, 0)
            dve.wait_ge(conv_loaded, CONV_LOADS)
            dve.tensor_scalar(bn_ve, var, BN_EPS, None, ALU.add).then_inc(bn_ve_ready, 1)
            dve.wait_ge(weights_lo, 1)
            for t, i in PE_TAPS:
                op = dve.tensor_scalar(diagonal(t, i), ident, weight(t, i), None, ALU.mult)
            op.then_inc(diagonals_ready, 1)
            conv_taps(0, images(0, FIRST_A["raw_q"]), None, 0, FIRST_WEIGHTS)
            dve.wait_ge(weights_hi, 2)
            dve.tensor_tensor(fg_lo[:], fg_st, fg_hi[:].bitcast(F32), ALU.subtract).then_inc(weights_lo, 1)
            dve.wait_ge(bn_rstd_ready, 1)
            dve.tensor_tensor(bn_scale, bn_tmp, gamma, ALU.mult).then_inc(dve_step, 1)
            dve.wait_ge(dve_step, 1)
            dve.tensor_tensor(bn_tmp, bn_scale, mean, ALU.mult).then_inc(dve_step, 1)
            dve.wait_ge(dve_step, 2)
            dve.tensor_tensor(bn_shift, beta, bn_tmp, ALU.subtract).then_inc(bn_ready, 1)
            dve.wait_ge(w_loaded, W_LOADS)
            dve.wait_ge(oh_full, 2)
            dve.tensor_tensor(oh_b, ps[:, 5, 0:CK], o_b, ALU.add).then_inc(pv_free, pv_count(0, 0))
            dve.wait_ge(weights_lo, 2)
            conv_taps(0, images(0, FIRST_A["raw_q"]), None, FIRST_WEIGHTS, FIRST_TAPS)
            scores(FIRST_D["sc_raw"], 0)
            outputs(FIRST_D["out_raw"], FIRST_D["out_raw"], PREP_STEPS, None)
            conv_taps(0, images(0, FIRST_A["raw_q"]), None, FIRST_TAPS, DVE_TAPS - CARRY)
            with dve.Fori(0, B - 1) as b:
                body(b, True)
            body(B - 1, False)

        @block.gpsimd
        def _(pool):
            def rstd(b, c):
                pool.wait_ge(var_ready, CK * b + c + 1)
                pool.tensor_tensor(stat_rstd[:, c:c + 1], stat_ve[:, c:c + 1], minus_half[:, c:c + 1],
                                   ALU.pow).then_inc(rstd_ready, 1)

            def add(total, m, i):
                total, product = inner(square(total), i), inner(square(prod[:, m % PROD_BUFS, :]), i)
                pool.tensor_tensor(total, total, product, ALU.add).then_inc(conv_pool, 1)

            def conv_adds(b, first, last):
                batch_0 = isinstance(b, int) and b == 0
                seq, adds = (FIRST_POOL_SEQ, FIRST_ADD_SEQ) if batch_0 else (POOL_SEQ, ADD_SEQ)
                for m in range(first, min(last, len(adds))):
                    t, i = adds[m]
                    n = seq.index((t, i)) + 1
                    pool.wait_ge(prod_ready, n if batch_0 else product_count(b, n))
                    if (t, i - 1) in adds:
                        before = adds.index((t, i - 1)) + 1
                        pool.wait_ge(conv_pool, before if batch_0 else add_count(b, before))
                    add(conv[:, t, :], m, i)

            def late_adds(b):
                for m in range(LATE - 1):
                    pool.wait_ge(prod_ready, late_product_count(b, m + 2))
                    if m > 0:
                        pool.wait_ge(conv_pool, late_add_count(b, m))
                    add(late, m, LATE_SEQ[m + 1][1])

            pool.memset(raw[:], 0.0).then_inc(images_cleared, 1)
            pool.wait_ge(constants_set, 1)
            pool.wait_ge(bn_ve_ready, 1)
            pool.tensor_tensor(bn_tmp, bn_ve, minus_half, ALU.pow).then_inc(bn_rstd_ready, 1)
            conv_adds(0, 0, POOL_ADDS)
            with pool.Fori(0, B - 1) as b:
                split_lo(pool, b + 1)
                late_adds(b)
                conv_adds(b + 1, 0, RSTD_AT[0])
                rstd(b, 0)
                conv_adds(b + 1, RSTD_AT[0], RSTD_AT[1])
                rstd(b, 1)
                conv_adds(b + 1, RSTD_AT[1], POOL_ADDS)
            late_adds(B - 1)
            rstd(B - 1, 0)
            rstd(B - 1, 1)


def _partitioned(a, rows):
    return np.ascontiguousarray(np.moveaxis(a.reshape(rows, P, *a.shape[1:]), 0, 1))


def kernel(x, L0_conv_wq, L0_conv_wk, L0_conv_wv, L0_conv_dw_kernel, L0_conv_pw_kernel, L0_conv_proj_kernel,
           L0_conv_bn_gamma, L0_conv_bn_beta, L0_conv_bn_mean, L0_conv_bn_var, L1_conv_f_w, L1_conv_f_b,
           L1_conv_g_w, L1_conv_g_b, L1_conv_h_w, L1_conv_h_b, L1_conv_o_w, L1_conv_o_b):
    import concourse.bacc as bacc
    from concourse.bass_utils import run_bass_kernel_spmd

    a = np.asarray
    kind, head, d = np.meshgrid(np.arange(3), np.arange(HEADS), np.arange(D), indexing="ij")
    order = (3 * D * head + D * kind + d).reshape(-1)
    wqkv = np.concatenate([a(L0_conv_wq), a(L0_conv_wk), a(L0_conv_wv)], 0)[order]
    dw = a(L0_conv_dw_kernel).reshape(3 * C, NTAPS)[order]
    pw = a(L0_conv_pw_kernel).reshape(3 * C, D)[order]
    pw_bd = np.zeros((P, TILES, P), pw.dtype)
    for oc_ in range(P):
        g = oc_ // D * D
        pw_bd[g:g + D, :, oc_] = pw.reshape(TILES, P, D)[:, oc_, :].T
    masks = np.concatenate([np.eye(P), np.kron(np.eye(HPT), np.ones((D, D))), np.kron(np.eye(HPT), np.ones((D, 1)))],
                           1).astype(np.float32)
    arrays = {
        "x_dram": np.ascontiguousarray(a(x).reshape(B, CK, P, N).transpose(0, 2, 1, 3)),
        "wqkv_dram": _partitioned(np.ascontiguousarray(wqkv.T), CK),
        "dw_dram": _partitioned(dw, TILES),
        "pw_dram": pw_bd,
        "proj_dram": _partitioned(np.ascontiguousarray(a(L0_conv_proj_kernel).reshape(C, 2 * C).T), 2 * CK),
        "bn_dram": np.ascontiguousarray(np.stack([a(v).reshape(CK, P).T for v in (
            L0_conv_bn_gamma, L0_conv_bn_beta, L0_conv_bn_mean, L0_conv_bn_var)], 1)),
        "fg_dram": np.ascontiguousarray(np.stack([_partitioned(np.ascontiguousarray(a(w).T), CK) for w in (
            L1_conv_f_w, L1_conv_g_w)], 1)),
        "hw_dram": _partitioned(a(L1_conv_h_w), CK),
        "ow_dram": _partitioned(np.ascontiguousarray(a(L1_conv_o_w).T), CK),
        "l1b_dram": np.ascontiguousarray(np.stack([a(v).reshape(CK, P).T for v in (
            L1_conv_f_b, L1_conv_g_b, L1_conv_h_b, L1_conv_o_b)], 1)),
        "masks_dram": masks,
    }
    nc = bacc.Bacc("TRN2", target_bir_lowering=False, num_devices=1)
    ins = [nc.dram_tensor(n, v.shape, mybir.dt.from_np(v.dtype), kind="ExternalInput").ap() for n, v in arrays.items()]
    out = nc.dram_tensor("out_dram", (B, P, CK, N), F32, kind="ExternalOutput").ap()
    x_ap, wqkv_ap, dw_ap, pw_ap, proj_ap, bn_ap, fg_ap, hw_ap, ow_ap, l1b_ap, masks_ap = ins
    conv_seq_kernel(nc, x_ap, wqkv_ap, dw_ap, pw_ap, proj_ap, bn_ap, fg_ap, hw_ap, ow_ap, l1b_ap, masks_ap, out)
    r = run_bass_kernel_spmd(nc, [arrays], core_ids=[0])
    got = r.results[0]["out_dram"]
    return np.ascontiguousarray(got.transpose(0, 2, 1, 3)).reshape(B, C, SIDE, SIDE)
```
